# Optimizing a Trainium2 kernel written in Bass

```python
import numpy as np
import jax
import jax.numpy as jnp

def _softmax(x, axis=-1):
    return jax.nn.softmax(x, axis=axis)

def _gelu(x):
    return jax.nn.gelu(x, approximate=True)

def _silu(x):
    return jax.nn.silu(x)

def _sigmoid(x):
    return jax.nn.sigmoid(x)

def _layernorm(x, axis=-1, eps=1e-05):
    m = jnp.mean(x, axis=axis, keepdims=True)
    v = jnp.var(x, axis=axis, keepdims=True)
    return (x - m) / jnp.sqrt(v + eps)

def _scatter_add(tgt, idx, src, axis=0):
    return tgt.at[idx].add(src)

def _segment_sum(src, seg, n):
    return jax.ops.segment_sum(src, seg, n)
kernel_name = 'mk_lm_tower_d4_tok_ids256_r4_7a4506'

def setup_inputs(seed: int=0):
    np.random.seed(seed)
    _w = jnp.asarray

    def _rec_inputs():
        import jax
        import jax.numpy as jnp
        _rk = jax.random.key(seed)
        x = jax.random.randint(jax.random.fold_in(_rk, 1), (64, 256), 0, 64, jnp.int32)
        itok_BS_0_255 = jax.random.randint(jax.random.fold_in(_rk, 21), (64, 256), 0, 64, jnp.int32)
        itok_BS_0_511 = jax.random.randint(jax.random.fold_in(_rk, 22), (64, 256), 0, 128, jnp.int32)
        itok_BS_0_127 = jax.random.randint(jax.random.fold_in(_rk, 23), (64, 256), 0, 128, jnp.int32)
        itok_BS_0_63 = jax.random.randint(jax.random.fold_in(_rk, 24), (64, 256), 0, 64, jnp.int32)
        itok_BS_0_3 = jax.random.randint(jax.random.fold_in(_rk, 25), (64, 256), 0, 4, jnp.int32)
        return (x, itok_BS_0_255, itok_BS_0_511, itok_BS_0_127, itok_BS_0_63, itok_BS_0_3)
    x, itok_BS_0_255, itok_BS_0_511, itok_BS_0_127, itok_BS_0_63, itok_BS_0_3 = _rec_inputs()

    def _L0_tok_setup():
        import jax, jax.numpy as jnp
        import numpy as np
        B, S = (128, 512)
        D_OUT = 64
        EMB = 16
        EPS_W = 1e-08
        EPS_LN = 1e-05

        def ternary_linear(x, W, b):
            scale = jnp.mean(jnp.abs(W))
            w_q = jnp.clip(jnp.round(W / (scale + EPS_W)), -1.0, 1.0) * scale
            w_eff = W + jax.lax.stop_gradient(w_q - W)
            return jnp.einsum('bsk,ok->bso', x, w_eff) + b

        def layer_norm(x, gamma, beta):
            mu = jnp.mean(x, axis=-1, keepdims=True)
            var = jnp.mean(jnp.square(x - mu), axis=-1, keepdims=True)
            return (x - mu) * jax.lax.rsqrt(var + EPS_LN) * gamma + beta
        key = jax.random.key(seed)
        ks = jax.random.split(key, 16)
        vocabs = {'event_type': 64, 'fault_class': 64, 'syscall_class': 128, 'opcode_family': 128, 'transition_type': 64, 'result_class': 4}
        inp = {}
        for i, (name, v) in enumerate(vocabs.items()):
            inp[name] = jax.random.randint(ks[i], (B, S), 0, v, dtype=jnp.int64)
        inp['E_et'] = jax.random.normal(ks[6], (64, EMB), dtype=jnp.float32)
        inp['E_fc'] = jax.random.normal(ks[7], (64, EMB), dtype=jnp.float32)
        inp['E_sc'] = jax.random.normal(ks[8], (128, EMB), dtype=jnp.float32)
        inp['E_of'] = jax.random.normal(ks[9], (128, EMB), dtype=jnp.float32)
        inp['E_tt'] = jax.random.normal(ks[10], (64, EMB), dtype=jnp.float32)
        inp['E_rc'] = jax.random.normal(ks[11], (4, EMB), dtype=jnp.float32)
        inp['W'] = jax.random.normal(ks[12], (D_OUT, 96), dtype=jnp.float32) * 0.1
        inp['b'] = jnp.zeros((D_OUT,), dtype=jnp.float32)
        inp['gamma'] = jnp.ones((D_OUT,), dtype=jnp.float32)
        inp['beta'] = jnp.zeros((D_OUT,), dtype=jnp.float32)
        return inp
    _L0_tok_all = _L0_tok_setup()
    _L0_tok_in = {k: v for k, v in _L0_tok_all.items() if k in ('E_et', 'E_fc', 'E_sc', 'E_of', 'E_tt', 'E_rc', 'W', 'b', 'gamma', 'beta')}
    del _L0_tok_all

    def _L0_attn_setup():
        import jax, jax.numpy as jnp
        import numpy as np
        key = jax.random.key(seed)
        k1, k2, k3 = jax.random.split(key, 3)
        d = 64
        x = jax.random.normal(k1, (8, 512, d), dtype=jnp.float32)
        Wq = jax.random.normal(k2, (d, d), dtype=jnp.float32) * d ** (-0.5)
        Wk = jax.random.normal(k3, (d, d), dtype=jnp.float32) * d ** (-0.5)
        return {'x': x, 'Wq': Wq, 'Wk': Wk}
    _L0_attn_all = _L0_attn_setup()
    _L0_attn_in = {k: v for k, v in _L0_attn_all.items() if k in ('Wq', 'Wk')}
    del _L0_attn_all

    def _L0_ffn_setup():
        import jax, jax.numpy as jnp
        import numpy as np
        E = 8
        K = 2
        D = 64
        H = 128
        DOUT = 64
        EPS = 1e-05
        key = jax.random.key(seed)
        ks = jax.random.split(key, 9)
        s = 0.02
        return {'x': jax.random.normal(ks[0], (4, 2048, D), jnp.float32), 'gamma': 1.0 + 0.05 * jax.random.normal(ks[1], (D,), jnp.float32), 'beta': 0.05 * jax.random.normal(ks[2], (D,), jnp.float32), 'Wr': 0.01 * jax.random.normal(ks[3], (D, E), jnp.float32), 'br': jnp.zeros((E,), jnp.float32), 'W1': s * jax.random.normal(ks[4], (E, D, H), jnp.float32), 'b1': s * jax.random.normal(ks[5], (E, H), jnp.float32), 'W2': s * jax.random.normal(ks[6], (E, H, DOUT), jnp.float32), 'b2': s * jax.random.normal(ks[7], (E, DOUT), jnp.float32)}
    _L0_ffn_all = _L0_ffn_setup()
    _L0_ffn_in = {k: v for k, v in _L0_ffn_all.items() if k in ('gamma', 'beta', 'Wr', 'br', 'W1', 'b1', 'W2', 'b2')}
    del _L0_ffn_all

    def _L1_attn_setup():
        import jax, jax.numpy as jnp
        import numpy as np
        B, L, E = (2, 2048, 64)
        H, K, DIL = (8, 31, 2)
        DH = E // H

        def neighbor_indices(length, k, d):
            i = jnp.arange(length)
            g = i % d
            p = i // d
            lg = (length - g + d - 1) // d
            start = jnp.clip(p - k // 2, 0, lg - k)
            t = jnp.arange(k)
            return g[:, None] + (start[:, None] + t[None, :]) * d
        key = jax.random.key(seed)
        k0, k1, k2 = jax.random.split(key, 3)
        s = 0.02
        return {'x': jax.random.normal(k0, (B, L, E), jnp.float32), 'w_qkv': jax.random.normal(k1, (E, 3 * E), jnp.float32) * s, 'b_qkv': jnp.zeros((3 * E,), jnp.float32), 'w_proj': jax.random.normal(k2, (E, E), jnp.float32) * s, 'b_proj': jnp.zeros((E,), jnp.float32)}
    _L1_attn_all = _L1_attn_setup()
    _L1_attn_in = {k: v for k, v in _L1_attn_all.items() if k in ('w_qkv', 'b_qkv', 'w_proj', 'b_proj')}
    del _L1_attn_all

    def _L1_ffn_setup():
        import math
        import jax, jax.numpy as jnp
        import numpy as np
        CAPACITY_FACTOR = 1.25
        TOP_K = 2
        LN_EPS = 1e-05

        def _layer_norm(x, gamma, beta):
            mu = jnp.mean(x, axis=-1, keepdims=True)
            var = jnp.var(x, axis=-1, keepdims=True)
            return (x - mu) * jax.lax.rsqrt(var + LN_EPS) * gamma + beta
        key = jax.random.key(seed)
        ks = jax.random.split(key, 4)
        B, S, D, F, E = (8, 1024, 64, 128, 8)
        x = jax.random.normal(ks[0], (B, S, D), dtype=jnp.float32)
        Wr = jax.random.normal(ks[1], (D, E), dtype=jnp.float32) / np.sqrt(D)
        br = jnp.zeros((E,), jnp.float32)
        W1 = jax.random.normal(ks[2], (E, D, F), dtype=jnp.float32) / np.sqrt(D)
        b1 = jnp.zeros((E, F), jnp.float32)
        W2 = jax.random.normal(ks[3], (E, F, D), dtype=jnp.float32) / np.sqrt(F)
        b2 = jnp.zeros((E, D), jnp.float32)
        gamma = jnp.ones((D,), jnp.float32)
        beta = jnp.zeros((D,), jnp.float32)
        return {'x': x, 'Wr': Wr, 'br': br, 'W1': W1, 'b1': b1, 'W2': W2, 'b2': b2, 'gamma': gamma, 'beta': beta}
    _L1_ffn_all = _L1_ffn_setup()
    _L1_ffn_in = {k: v for k, v in _L1_ffn_all.items() if k in ('Wr', 'br', 'W1', 'b1', 'W2', 'b2', 'gamma', 'beta')}
    del _L1_ffn_all

    def _L2_attn_setup():
        import jax, jax.numpy as jnp
        import numpy as np
        IN_C = 64
        HID_C = 64
        HEADS = 8
        SCALE = 1.0 / np.sqrt(HID_C / HEADS).astype(np.float32)
        key = jax.random.key(seed)
        k_v, k_q, k_k, k_w, k_o, k_b = jax.random.split(key, 6)
        B, S = (4, 512)
        lim_in = 1.0 / np.sqrt(IN_C)
        lim_out = 1.0 / np.sqrt(IN_C * HEADS)
        v = jax.random.normal(k_v, (B, S, IN_C), dtype=jnp.float32)
        WQ = jax.random.uniform(k_q, (IN_C, IN_C * HEADS), jnp.float32, -lim_in, lim_in)
        WK = jax.random.uniform(k_k, (IN_C, IN_C * HEADS), jnp.float32, -lim_in, lim_in)
        WV = jax.random.uniform(k_w, (IN_C, IN_C * HEADS), jnp.float32, -lim_in, lim_in)
        Wout = jax.random.uniform(k_o, (IN_C * HEADS, HID_C), jnp.float32, -lim_out, lim_out)
        bout = jax.random.uniform(k_b, (HID_C,), jnp.float32, -lim_out, lim_out)
        return {'v': v, 'WQ': WQ, 'WK': WK, 'WV': WV, 'Wout': Wout, 'bout': bout}
    _L2_attn_all = _L2_attn_setup()
    _L2_attn_in = {k: v for k, v in _L2_attn_all.items() if k in ('WQ', 'WK', 'WV', 'Wout', 'bout')}
    del _L2_attn_all

    def _L2_ffn_setup():
        import jax, jax.numpy as jnp
        import numpy as np
        B, N, D = (16, 1024, 64)
        NUM_EXPERTS, TOP_K, HEADS = (4, 2, 4)
        N_EDGES = 262144
        LN_EPS = 1e-05

        def _layernorm(x, g, b):
            mu = x.mean(-1, keepdims=True)
            var = ((x - mu) ** 2).mean(-1, keepdims=True)
            return (x - mu) * jax.lax.rsqrt(var + LN_EPS) * g + b

        def _forward(x, edge_index, W_gat, att_src, att_dst, b_gat, ln_gamma, ln_beta, W1, b1, W2, b2):
            Bc, Nc, Dc = x.shape
            M = Bc * Nc
            x_flat = x.reshape(M, Dc)
            h = (x_flat @ W_gat).reshape(M, HEADS, NUM_EXPERTS)
            loops = jnp.arange(M, dtype=edge_index.dtype)
            src = jnp.concatenate([edge_index[0], loops])
            dst = jnp.concatenate([edge_index[1], loops])
            a_src = (h * att_src).sum(-1)
            a_dst = (h * att_dst).sum(-1)
            e = jax.nn.leaky_relu(a_src[src] + a_dst[dst], negative_slope=0.2)
            e_max = jax.ops.segment_max(e, dst, num_segments=M)
            ee = jnp.exp(e - e_max[dst])
            denom = jax.ops.segment_sum(ee, dst, num_segments=M)
            alpha = ee / (denom[dst] + 1e-16)
            msg = h[src] * alpha[:, :, None]
            agg = jax.ops.segment_sum(msg, dst, num_segments=M).reshape(M, HEADS * NUM_EXPERTS) + b_gat
            scores = _layernorm(agg, ln_gamma, ln_beta).reshape(M, HEADS, NUM_EXPERTS).mean(1)
            scores = scores.reshape(Bc, Nc, NUM_EXPERTS)
            topk_s, topk_i = jax.lax.top_k(scores, TOP_K)
            w = jax.nn.softmax(topk_s, axis=-1)
            out = jnp.zeros_like(x)
            for ei in range(NUM_EXPERTS):
                g = jnp.where(topk_i == ei, w, 0.0).sum(-1)
                hh = jax.nn.gelu(x @ W1[ei] + b1[ei], approximate=False)
                out = out + g[..., None] * (hh @ W2[ei] + b2[ei])
            return out
        key = jax.random.key(seed)
        ks = jax.random.split(key, 8)
        s = 0.05
        return {'x': jax.random.normal(ks[0], (B, N, D), jnp.float32), 'W_gat': jax.random.normal(ks[1], (D, HEADS * NUM_EXPERTS), jnp.float32) * s, 'att_src': jax.random.normal(ks[2], (HEADS, NUM_EXPERTS), jnp.float32) * s, 'att_dst': jax.random.normal(ks[3], (HEADS, NUM_EXPERTS), jnp.float32) * s, 'b_gat': jnp.zeros((HEADS * NUM_EXPERTS,), jnp.float32), 'ln_gamma': jnp.ones((HEADS * NUM_EXPERTS,), jnp.float32), 'ln_beta': jnp.zeros((HEADS * NUM_EXPERTS,), jnp.float32), 'W1': jax.random.normal(ks[4], (NUM_EXPERTS, D, 2 * D), jnp.float32) * s, 'b1': jnp.zeros((NUM_EXPERTS, 2 * D), jnp.float32), 'W2': jax.random.normal(ks[5], (NUM_EXPERTS, 2 * D, D), jnp.float32) * s, 'b2': jnp.zeros((NUM_EXPERTS, D), jnp.float32), 'edge_index': jax.random.randint(ks[6], (2, N_EDGES), 0, B * N, jnp.int32)}
    _L2_ffn_all = _L2_ffn_setup()
    _L2_ffn_in = {k: v for k, v in _L2_ffn_all.items() if k in ('W_gat', 'att_src', 'att_dst', 'b_gat', 'ln_gamma', 'ln_beta', 'W1', 'b1', 'W2', 'b2', 'edge_index')}
    del _L2_ffn_all

    def _L3_attn_setup():
        import jax, jax.numpy as jnp
        import numpy as np
        import math
        CHUNK = 128

        def _build_slopes(n):

            def p2(n):
                start = 2.0 ** (-2.0 ** (-(math.log2(n) - 3)))
                return [start ** (i + 1) for i in range(n)]
            if math.log2(n).is_integer():
                s = p2(n)
            else:
                c = 2 ** math.floor(math.log2(n))
                s = p2(c) + p2(2 * c)[0::2][:n - c]
            return np.asarray(s, dtype=np.float32)

        def _lightning_attn(q, k, v, slopes):
            b, h, l, d = q.shape
            n = l // CHUNK
            s = slopes.reshape(h, 1, 1)
            pos = jnp.arange(CHUNK, dtype=q.dtype)
            diff = pos[:, None] - pos[None, :]
            mask = jnp.where(diff >= 0, jnp.exp(-s * diff), 0.0)[None]
            q_dec = jnp.exp(-slopes[:, None] * pos)[None, :, :, None]
            k_dec = jnp.exp(-slopes[:, None] * (CHUNK - pos))[None, :, :, None]
            blk = jnp.exp(-slopes * CHUNK).reshape(1, h, 1, 1)
            qc = q.reshape(b, h, n, CHUNK, d).transpose(2, 0, 1, 3, 4)
            kc = k.reshape(b, h, n, CHUNK, d).transpose(2, 0, 1, 3, 4)
            vc = v.reshape(b, h, n, CHUNK, d).transpose(2, 0, 1, 3, 4)

            def step(S, xs):
                qi, ki, vi = xs
                scores = jnp.einsum('bhcd,bhed->bhce', qi, ki) * mask
                intra = jnp.einsum('bhce,bhed->bhcd', scores, vi)
                inter = jnp.einsum('bhcd,bhde->bhce', qi * q_dec, S)
                S_new = blk * S + jnp.einsum('bhcd,bhce->bhde', ki * k_dec, vi)
                return (S_new, intra + inter)
            S0 = jnp.zeros((b, h, d, d), q.dtype)
            _, o = jax.lax.scan(step, S0, (qc, kc, vc))
            return o.transpose(1, 2, 0, 3, 4).reshape(b, h, l, d)
        key = jax.random.key(seed)
        k1, k2, k3 = jax.random.split(key, 3)
        b, l, c, h = (8, 4096, 64, 8)
        x = jax.random.normal(k1, (b, l, c), dtype=jnp.float32)
        w_qkv = jax.random.normal(k2, (c, 3 * c), dtype=jnp.float32) * 0.02
        w_proj = jax.random.normal(k3, (c, c), dtype=jnp.float32) * 0.02
        b_proj = jnp.zeros((c,), dtype=jnp.float32)
        slopes = jnp.asarray(_build_slopes(h))
        return {'x': x, 'w_qkv': w_qkv, 'w_proj': w_proj, 'b_proj': b_proj, 'slopes': slopes}
    _L3_attn_all = _L3_attn_setup()
    _L3_attn_in = {k: v for k, v in _L3_attn_all.items() if k in ('w_qkv', 'w_proj', 'b_proj', 'slopes')}
    del _L3_attn_all

    def _L3_ffn_setup():
        import jax, jax.numpy as jnp
        import numpy as np
        D_MODEL = 64
        N_EXPERTS = 16
        HIDDEN = 128
        SCALE = 0.02
        key = jax.random.key(seed)
        ks = jax.random.split(key, 5)
        x = jax.random.normal(ks[0], (4, 2048, D_MODEL), dtype=jnp.float32)
        gate_w = jax.random.normal(ks[1], (D_MODEL, N_EXPERTS), dtype=jnp.float32) * SCALE
        gate_b = jnp.zeros((N_EXPERTS,), dtype=jnp.float32)
        w1 = jax.random.normal(ks[2], (N_EXPERTS, D_MODEL, HIDDEN), dtype=jnp.float32) * SCALE
        w2 = jax.random.normal(ks[3], (N_EXPERTS, D_MODEL, HIDDEN), dtype=jnp.float32) * SCALE
        w3 = jax.random.normal(ks[4], (N_EXPERTS, HIDDEN, D_MODEL), dtype=jnp.float32) * SCALE
        return {'x': x, 'gate_w': gate_w, 'gate_b': gate_b, 'w1': w1, 'w2': w2, 'w3': w3}
    _L3_ffn_all = _L3_ffn_setup()
    _L3_ffn_in = {k: v for k, v in _L3_ffn_all.items() if k in ('gate_w', 'gate_b', 'w1', 'w2', 'w3')}
    del _L3_ffn_all
    return {'x': x, 'itok_BS_0_255': itok_BS_0_255, 'itok_BS_0_511': itok_BS_0_511, 'itok_BS_0_127': itok_BS_0_127, 'itok_BS_0_63': itok_BS_0_63, 'itok_BS_0_3': itok_BS_0_3, 'L0_tok_E_et': _L0_tok_in['E_et'], 'L0_tok_E_fc': _L0_tok_in['E_fc'], 'L0_tok_E_sc': _L0_tok_in['E_sc'], 'L0_tok_E_of': _L0_tok_in['E_of'], 'L0_tok_E_tt': _L0_tok_in['E_tt'], 'L0_tok_E_rc': _L0_tok_in['E_rc'], 'L0_tok_W': _L0_tok_in['W'], 'L0_tok_b': _L0_tok_in['b'], 'L0_tok_gamma': _L0_tok_in['gamma'], 'L0_tok_beta': _L0_tok_in['beta'], 'L0_attn_Wq': _L0_attn_in['Wq'], 'L0_attn_Wk': _L0_attn_in['Wk'], 'L0_ffn_gamma': _L0_ffn_in['gamma'], 'L0_ffn_beta': _L0_ffn_in['beta'], 'L0_ffn_Wr': _L0_ffn_in['Wr'], 'L0_ffn_br': _L0_ffn_in['br'], 'L0_ffn_W1': _L0_ffn_in['W1'], 'L0_ffn_b1': _L0_ffn_in['b1'], 'L0_ffn_W2': _L0_ffn_in['W2'], 'L0_ffn_b2': _L0_ffn_in['b2'], 'L1_attn_w_qkv': _L1_attn_in['w_qkv'], 'L1_attn_b_qkv': _L1_attn_in['b_qkv'], 'L1_attn_w_proj': _L1_attn_in['w_proj'], 'L1_attn_b_proj': _L1_attn_in['b_proj'], 'L1_ffn_Wr': _L1_ffn_in['Wr'], 'L1_ffn_br': _L1_ffn_in['br'], 'L1_ffn_W1': _L1_ffn_in['W1'], 'L1_ffn_b1': _L1_ffn_in['b1'], 'L1_ffn_W2': _L1_ffn_in['W2'], 'L1_ffn_b2': _L1_ffn_in['b2'], 'L1_ffn_gamma': _L1_ffn_in['gamma'], 'L1_ffn_beta': _L1_ffn_in['beta'], 'L2_attn_WQ': _L2_attn_in['WQ'], 'L2_attn_WK': _L2_attn_in['WK'], 'L2_attn_WV': _L2_attn_in['WV'], 'L2_attn_Wout': _L2_attn_in['Wout'], 'L2_attn_bout': _L2_attn_in['bout'], 'L2_ffn_W_gat': _L2_ffn_in['W_gat'], 'L2_ffn_att_src': _L2_ffn_in['att_src'], 'L2_ffn_att_dst': _L2_ffn_in['att_dst'], 'L2_ffn_b_gat': _L2_ffn_in['b_gat'], 'L2_ffn_ln_gamma': _L2_ffn_in['ln_gamma'], 'L2_ffn_ln_beta': _L2_ffn_in['ln_beta'], 'L2_ffn_W1': _L2_ffn_in['W1'], 'L2_ffn_b1': _L2_ffn_in['b1'], 'L2_ffn_W2': _L2_ffn_in['W2'], 'L2_ffn_b2': _L2_ffn_in['b2'], 'L2_ffn_edge_index': _L2_ffn_in['edge_index'], 'L3_attn_w_qkv': _L3_attn_in['w_qkv'], 'L3_attn_w_proj': _L3_attn_in['w_proj'], 'L3_attn_b_proj': _L3_attn_in['b_proj'], 'L3_attn_slopes': _L3_attn_in['slopes'], 'L3_ffn_gate_w': _L3_ffn_in['gate_w'], 'L3_ffn_gate_b': _L3_ffn_in['gate_b'], 'L3_ffn_w1': _L3_ffn_in['w1'], 'L3_ffn_w2': _L3_ffn_in['w2'], 'L3_ffn_w3': _L3_ffn_in['w3']}

def reference(x, itok_BS_0_255, itok_BS_0_511, itok_BS_0_127, itok_BS_0_63, itok_BS_0_3, L0_tok_E_et, L0_tok_E_fc, L0_tok_E_sc, L0_tok_E_of, L0_tok_E_tt, L0_tok_E_rc, L0_tok_W, L0_tok_b, L0_tok_gamma, L0_tok_beta, L0_attn_Wq, L0_attn_Wk, L0_ffn_gamma, L0_ffn_beta, L0_ffn_Wr, L0_ffn_br, L0_ffn_W1, L0_ffn_b1, L0_ffn_W2, L0_ffn_b2, L1_attn_w_qkv, L1_attn_b_qkv, L1_attn_w_proj, L1_attn_b_proj, L1_ffn_Wr, L1_ffn_br, L1_ffn_W1, L1_ffn_b1, L1_ffn_W2, L1_ffn_b2, L1_ffn_gamma, L1_ffn_beta, L2_attn_WQ, L2_attn_WK, L2_attn_WV, L2_attn_Wout, L2_attn_bout, L2_ffn_W_gat, L2_ffn_att_src, L2_ffn_att_dst, L2_ffn_b_gat, L2_ffn_ln_gamma, L2_ffn_ln_beta, L2_ffn_W1, L2_ffn_b1, L2_ffn_W2, L2_ffn_b2, L2_ffn_edge_index, L3_attn_w_qkv, L3_attn_w_proj, L3_attn_b_proj, L3_attn_slopes, L3_ffn_gate_w, L3_ffn_gate_b, L3_ffn_w1, L3_ffn_w2, L3_ffn_w3):
    import jax
    import jax.numpy as jnp

    def _L0_tok_ref(event_type, fault_class, syscall_class, opcode_family, transition_type, result_class, E_et, E_fc, E_sc, E_of, E_tt, E_rc, W, b, gamma, beta):
        import jax, jax.numpy as jnp
        import numpy as np
        B, S = (128, 512)
        D_OUT = 64
        EMB = 16
        EPS_W = 1e-08
        EPS_LN = 1e-05

        def ternary_linear(x, W, b):
            scale = jnp.mean(jnp.abs(W))
            w_q = jnp.clip(jnp.round(W / (scale + EPS_W)), -1.0, 1.0) * scale
            w_eff = W + jax.lax.stop_gradient(w_q - W)
            return jnp.einsum('bsk,ok->bso', x, w_eff) + b

        def layer_norm(x, gamma, beta):
            mu = jnp.mean(x, axis=-1, keepdims=True)
            var = jnp.mean(jnp.square(x - mu), axis=-1, keepdims=True)
            return (x - mu) * jax.lax.rsqrt(var + EPS_LN) * gamma + beta
        combined = jnp.concatenate([E_et[event_type], E_fc[fault_class], E_sc[syscall_class], E_of[opcode_family], E_tt[transition_type], E_rc[result_class]], axis=-1)
        z = ternary_linear(combined, W, b)
        return layer_norm(z, gamma, beta)

    def _L0_attn_ref(x, Wq, Wk):
        import jax, jax.numpy as jnp
        import numpy as np
        d = x.shape[-1]
        scale = d ** (-0.5)
        q = jnp.einsum('bnd,ed->bne', x, Wq)
        k = jnp.einsum('bnd,ed->bne', x, Wk)
        sim = jnp.einsum('bid,bjd->bij', q, k) * scale
        attn = jax.nn.softmax(sim, axis=-1)
        out = jnp.einsum('bij,bjd->bid', attn, x)
        return out

    def _L0_ffn_ref(x, gamma, beta, Wr, br, W1, b1, W2, b2):
        import jax, jax.numpy as jnp
        import numpy as np
        E = 8
        K = 2
        D = 64
        H = 128
        DOUT = 64
        EPS = 1e-05
        mu = jnp.mean(x, axis=-1, keepdims=True)
        var = jnp.mean(jnp.square(x - mu), axis=-1, keepdims=True)
        xn = (x - mu) * jax.lax.rsqrt(var + EPS) * gamma + beta
        logits = jnp.einsum('bsd,de->bse', xn, Wr) + br
        top_vals, top_idx = jax.lax.top_k(logits, K)
        w = jax.nn.softmax(top_vals, axis=-1)
        w_full = jnp.einsum('bsk,bske->bse', w, jax.nn.one_hot(top_idx, E, dtype=w.dtype))
        y = jnp.zeros(x.shape[:-1] + (DOUT,), x.dtype)
        for e in range(E):
            h = jax.nn.gelu(jnp.einsum('bsd,dh->bsh', xn, W1[e]) + b1[e], approximate=False)
            y_e = jnp.einsum('bsh,hd->bsd', h, W2[e]) + b2[e]
            y = y + y_e * w_full[..., e, None]
        return y

    def _L1_attn_ref(x, w_qkv, b_qkv, w_proj, b_proj):
        import jax, jax.numpy as jnp
        import numpy as np
        B, L, E = (2, 2048, 64)
        H, K, DIL = (8, 31, 2)
        DH = E // H

        def neighbor_indices(length, k, d):
            i = jnp.arange(length)
            g = i % d
            p = i // d
            lg = (length - g + d - 1) // d
            start = jnp.clip(p - k // 2, 0, lg - k)
            t = jnp.arange(k)
            return g[:, None] + (start[:, None] + t[None, :]) * d
        b, l, e = x.shape
        qkv = (x @ w_qkv + b_qkv).reshape(b, l, 3, H, DH)
        q, k, v = (qkv[:, :, 0], qkv[:, :, 1], qkv[:, :, 2])
        nbr = neighbor_indices(l, K, DIL)
        kg = k[:, nbr]
        vg = v[:, nbr]
        scale = DH ** (-0.5)
        attn = jnp.einsum('blhd,blkhd->blhk', q, kg) * scale
        attn = jax.nn.softmax(attn, axis=-1)
        out = jnp.einsum('blhk,blkhd->blhd', attn, vg).reshape(b, l, e)
        return out @ w_proj + b_proj

    def _L1_ffn_ref(x, Wr, br, W1, b1, W2, b2, gamma, beta):
        import math
        import jax, jax.numpy as jnp
        import numpy as np
        CAPACITY_FACTOR = 1.25
        TOP_K = 2
        LN_EPS = 1e-05

        def _layer_norm(x, gamma, beta):
            mu = jnp.mean(x, axis=-1, keepdims=True)
            var = jnp.var(x, axis=-1, keepdims=True)
            return (x - mu) * jax.lax.rsqrt(var + LN_EPS) * gamma + beta
        B, S, D = x.shape
        E = Wr.shape[1]
        N = B * S
        K = TOP_K
        logits = jnp.mean(x, axis=1) @ Wr + br
        routing_weights = jax.nn.softmax(logits, axis=-1)
        capacity = float(math.ceil(N * CAPACITY_FACTOR / E))
        expected_loads = routing_weights.sum(axis=0) * (N / B)
        scale = jnp.where(expected_loads > capacity, capacity / expected_loads, 1.0)
        routing_weights = jax.nn.softmax(routing_weights * scale, axis=-1)
        rw_tok = jnp.broadcast_to(routing_weights[:, None, :], (B, S, E)).reshape(N, E)
        top_w, top_i = jax.lax.top_k(rw_tok, K)
        top_w = jax.nn.softmax(top_w, axis=-1)
        xf = x.reshape(N, D)
        h = jax.nn.gelu(jnp.einsum('nd,edf->enf', xf, W1) + b1[:, None, :], approximate=False)
        y = jnp.einsum('enf,efd->end', h, W2) + b2[:, None, :]
        w_dense = jnp.zeros((N, E), x.dtype).at[jnp.arange(N)[:, None], top_i].add(top_w)
        out = jnp.einsum('ne,end->nd', w_dense, y).reshape(B, S, D)
        out = _layer_norm(out + x, gamma, beta)
        return out

    def _L2_attn_ref(v, WQ, WK, WV, Wout, bout):
        import jax, jax.numpy as jnp
        import numpy as np
        IN_C = 64
        HID_C = 64
        HEADS = 8
        SCALE = 1.0 / np.sqrt(HID_C / HEADS).astype(np.float32)
        B, S, C = v.shape
        H = HEADS
        q = (v @ WQ).reshape(B, S, H, C)
        k = (v @ WK).reshape(B, S, H, C)
        val = (v @ WV).reshape(B, S, H, C)
        scores = jnp.einsum('bshc,bthc->bsth', q, k) * SCALE
        A = jax.nn.softmax(scores, axis=2)
        u = jnp.einsum('bsth,bthc->bshc', A, val).reshape(B, S, H * C)
        return u @ Wout + bout

    def _L2_ffn_ref(x, W_gat, att_src, att_dst, b_gat, ln_gamma, ln_beta, W1, b1, W2, b2, edge_index):
        import jax, jax.numpy as jnp
        import numpy as np
        B, N, D = (16, 1024, 64)
        NUM_EXPERTS, TOP_K, HEADS = (4, 2, 4)
        N_EDGES = 262144
        LN_EPS = 1e-05

        def _layernorm(x, g, b):
            mu = x.mean(-1, keepdims=True)
            var = ((x - mu) ** 2).mean(-1, keepdims=True)
            return (x - mu) * jax.lax.rsqrt(var + LN_EPS) * g + b

        def _forward(x, edge_index, W_gat, att_src, att_dst, b_gat, ln_gamma, ln_beta, W1, b1, W2, b2):
            Bc, Nc, Dc = x.shape
            M = Bc * Nc
            x_flat = x.reshape(M, Dc)
            h = (x_flat @ W_gat).reshape(M, HEADS, NUM_EXPERTS)
            loops = jnp.arange(M, dtype=edge_index.dtype)
            src = jnp.concatenate([edge_index[0], loops])
            dst = jnp.concatenate([edge_index[1], loops])
            a_src = (h * att_src).sum(-1)
            a_dst = (h * att_dst).sum(-1)
            e = jax.nn.leaky_relu(a_src[src] + a_dst[dst], negative_slope=0.2)
            e_max = jax.ops.segment_max(e, dst, num_segments=M)
            ee = jnp.exp(e - e_max[dst])
            denom = jax.ops.segment_sum(ee, dst, num_segments=M)
            alpha = ee / (denom[dst] + 1e-16)
            msg = h[src] * alpha[:, :, None]
            agg = jax.ops.segment_sum(msg, dst, num_segments=M).reshape(M, HEADS * NUM_EXPERTS) + b_gat
            scores = _layernorm(agg, ln_gamma, ln_beta).reshape(M, HEADS, NUM_EXPERTS).mean(1)
            scores = scores.reshape(Bc, Nc, NUM_EXPERTS)
            topk_s, topk_i = jax.lax.top_k(scores, TOP_K)
            w = jax.nn.softmax(topk_s, axis=-1)
            out = jnp.zeros_like(x)
            for ei in range(NUM_EXPERTS):
                g = jnp.where(topk_i == ei, w, 0.0).sum(-1)
                hh = jax.nn.gelu(x @ W1[ei] + b1[ei], approximate=False)
                out = out + g[..., None] * (hh @ W2[ei] + b2[ei])
            return out
        return _forward(x, edge_index, W_gat, att_src, att_dst, b_gat, ln_gamma, ln_beta, W1, b1, W2, b2)

    def _L3_attn_ref(x, w_qkv, w_proj, b_proj, slopes):
        import jax, jax.numpy as jnp
        import numpy as np
        import math
        CHUNK = 128

        def _build_slopes(n):

            def p2(n):
                start = 2.0 ** (-2.0 ** (-(math.log2(n) - 3)))
                return [start ** (i + 1) for i in range(n)]
            if math.log2(n).is_integer():
                s = p2(n)
            else:
                c = 2 ** math.floor(math.log2(n))
                s = p2(c) + p2(2 * c)[0::2][:n - c]
            return np.asarray(s, dtype=np.float32)

        def _lightning_attn(q, k, v, slopes):
            b, h, l, d = q.shape
            n = l // CHUNK
            s = slopes.reshape(h, 1, 1)
            pos = jnp.arange(CHUNK, dtype=q.dtype)
            diff = pos[:, None] - pos[None, :]
            mask = jnp.where(diff >= 0, jnp.exp(-s * diff), 0.0)[None]
            q_dec = jnp.exp(-slopes[:, None] * pos)[None, :, :, None]
            k_dec = jnp.exp(-slopes[:, None] * (CHUNK - pos))[None, :, :, None]
            blk = jnp.exp(-slopes * CHUNK).reshape(1, h, 1, 1)
            qc = q.reshape(b, h, n, CHUNK, d).transpose(2, 0, 1, 3, 4)
            kc = k.reshape(b, h, n, CHUNK, d).transpose(2, 0, 1, 3, 4)
            vc = v.reshape(b, h, n, CHUNK, d).transpose(2, 0, 1, 3, 4)

            def step(S, xs):
                qi, ki, vi = xs
                scores = jnp.einsum('bhcd,bhed->bhce', qi, ki) * mask
                intra = jnp.einsum('bhce,bhed->bhcd', scores, vi)
                inter = jnp.einsum('bhcd,bhde->bhce', qi * q_dec, S)
                S_new = blk * S + jnp.einsum('bhcd,bhce->bhde', ki * k_dec, vi)
                return (S_new, intra + inter)
            S0 = jnp.zeros((b, h, d, d), q.dtype)
            _, o = jax.lax.scan(step, S0, (qc, kc, vc))
            return o.transpose(1, 2, 0, 3, 4).reshape(b, h, l, d)
        b, l, c = x.shape
        h = slopes.shape[0]
        d = c // h
        scale = d ** (-0.5)
        qkv = (x @ w_qkv).reshape(b, l, 3, h, d)
        q = qkv[:, :, 0].transpose(0, 2, 1, 3) * scale
        k = qkv[:, :, 1].transpose(0, 2, 1, 3)
        v = qkv[:, :, 2].transpose(0, 2, 1, 3)
        o = _lightning_attn(q, k, v, slopes)
        out = o.transpose(0, 2, 1, 3).reshape(b, l, c) @ w_proj + b_proj
        return out

    def _L3_ffn_ref(x, gate_w, gate_b, w1, w2, w3):
        import jax, jax.numpy as jnp
        import numpy as np
        D_MODEL = 64
        N_EXPERTS = 16
        HIDDEN = 128
        SCALE = 0.02
        n_experts = w1.shape[0]
        logits = jnp.einsum('bsd,de->bse', x, gate_w) + gate_b
        probs = jax.nn.softmax(logits, axis=-1)
        top_probs, top_idx = jax.lax.top_k(probs, 2)
        top_probs = top_probs / jnp.sum(top_probs, axis=-1, keepdims=True)
        dispatch = jnp.sum(jax.nn.one_hot(top_idx, n_experts, dtype=x.dtype) * top_probs[..., None], axis=-2)
        h1 = jnp.einsum('bsd,edh->bseh', x, w1)
        h2 = jnp.einsum('bsd,edh->bseh', x, w2)
        hidden = jax.nn.silu(h1) * h2
        expert_out = jnp.einsum('bseh,eho->bseo', hidden, w3)
        return jnp.einsum('bseo,bse->bso', expert_out, dispatch)
    h = _L0_tok_ref(x, itok_BS_0_255, itok_BS_0_511, itok_BS_0_127, itok_BS_0_63, itok_BS_0_3, L0_tok_E_et, L0_tok_E_fc, L0_tok_E_sc, L0_tok_E_of, L0_tok_E_tt, L0_tok_E_rc, L0_tok_W, L0_tok_b, L0_tok_gamma, L0_tok_beta)
    h = h + _L0_attn_ref(_layernorm(h, axis=-1), L0_attn_Wq, L0_attn_Wk)
    h = h + _L0_ffn_ref(_layernorm(h, axis=-1), L0_ffn_gamma, L0_ffn_beta, L0_ffn_Wr, L0_ffn_br, L0_ffn_W1, L0_ffn_b1, L0_ffn_W2, L0_ffn_b2)
    h = h + _L1_attn_ref(_layernorm(h, axis=-1), L1_attn_w_qkv, L1_attn_b_qkv, L1_attn_w_proj, L1_attn_b_proj)
    h = h + _L1_ffn_ref(_layernorm(h, axis=-1), L1_ffn_Wr, L1_ffn_br, L1_ffn_W1, L1_ffn_b1, L1_ffn_W2, L1_ffn_b2, L1_ffn_gamma, L1_ffn_beta)
    h = h + _L2_attn_ref(_layernorm(h, axis=-1), L2_attn_WQ, L2_attn_WK, L2_attn_WV, L2_attn_Wout, L2_attn_bout)
    h = h + _L2_ffn_ref(_layernorm(h, axis=-1), L2_ffn_W_gat, L2_ffn_att_src, L2_ffn_att_dst, L2_ffn_b_gat, L2_ffn_ln_gamma, L2_ffn_ln_beta, L2_ffn_W1, L2_ffn_b1, L2_ffn_W2, L2_ffn_b2, L2_ffn_edge_index)
    h = h + _L3_attn_ref(_layernorm(h, axis=-1), L3_attn_w_qkv, L3_attn_w_proj, L3_attn_b_proj, L3_attn_slopes)
    h = h + _L3_ffn_ref(_layernorm(h, axis=-1), L3_ffn_gate_w, L3_ffn_gate_b, L3_ffn_w1, L3_ffn_w2, L3_ffn_w3)
    return h

_drawn_inputs = setup_inputs


def setup_inputs(seed=0):
    import zlib

    import numpy as np

    out = dict(_drawn_inputs(seed))
    spreads = {'L0_tok_b': (0.0, 0.1),
     'L0_tok_gamma': (1.0, 0.2),
     'L0_tok_beta': (0.0, 0.1),
     'L0_ffn_br': (0.0, 0.47),
     'L1_attn_b_qkv': (0.0, 0.288),
     'L1_attn_b_proj': (0.0, 0.1),
     'L1_ffn_br': (0.0, 0.8),
     'L1_ffn_b1': (0.0, 0.35),
     'L1_ffn_b2': (0.0, 0.1),
     'L1_ffn_gamma': (1.0, 0.2),
     'L1_ffn_beta': (0.0, 0.1),
     'L2_ffn_b_gat': (0.0, 0.1),
     'L2_ffn_ln_gamma': (1.0, 0.6),
     'L2_ffn_ln_beta': (0.0, 2.0),
     'L2_ffn_b1': (0.0, 0.705),
     'L2_ffn_b2': (0.0, 0.1),
     'L3_attn_b_proj': (0.0, 0.502),
     'L3_ffn_gate_b': (0.0, 0.8)}
    factors = {'L0_ffn_gamma': 3.32,
     'L0_ffn_beta': 8.0,
     'L0_ffn_Wr': 3.184,
     'L0_ffn_W1': 4.809,
     'L0_ffn_b1': 8.0,
     'L0_ffn_W2': 5.301,
     'L0_ffn_b2': 4.175,
     'L2_attn_bout': 3.424,
     'L2_ffn_att_src': 28.613,
     'L2_ffn_att_dst': 48.379,
     'L3_attn_w_qkv': 8.0,
     'L3_attn_w_proj': 8.0,
     'L3_attn_slopes': 8.0,
     'L3_ffn_gate_w': 8.0,
     'L3_ffn_w1': 8.0,
     'L3_ffn_w2': 8.0,
     'L3_ffn_w3': 8.0,
     'L1_attn_w_qkv': 2.971}
    for name, (base, spread) in spreads.items():
        noise = np.random.default_rng([zlib.crc32(name.encode()), seed]).standard_normal(out[name].shape)
        drawn = base * np.exp(spread * noise) if base else spread * noise
        out[name] = jnp.asarray(drawn.astype(out[name].dtype))
    for name, factor in factors.items():
        out[name] = (out[name] * factor).astype(out[name].dtype)
    return out
```

```python
from contextlib import ExitStack

import concourse.bass as bass
from concourse import mybir

F32 = mybir.dt.float32
BF16 = mybir.dt.bfloat16
I32 = mybir.dt.int32
ACT = mybir.ActivationFunctionType
ALU = mybir.AluOpType
AX = mybir.AxisListType
ds = bass.ds

P = 128
D = 64
B, S = 64, 256
TOKENS = B * S
TILES = TOKENS // P
TPB = S // P
BIG = 1e30


def bc(ap, axis, n):
    shape = list(ap.shape)
    shape.insert(axis, n)
    return ap.unsqueeze(axis).broadcast_to(shape)


def wait_apart(eng, sem, value, passed):
    eng.wait_ge(sem, value)
    eng.sem_inc(passed, 1)


def chain(eng, sem, i=0, per=0, base=0):
    n = [0]

    def link(ins):
        n[0] += 1
        ins.then_inc(sem, 1)
        eng.wait_ge(sem, base + i * per + n[0])

    link.count = n
    return link


class Stage:

    def __init__(self, nc, name):
        self.nc, self.name = nc, name

    def __enter__(self):
        self.ctx, self.sems = ExitStack(), []
        self.ctx.__enter__()
        return self

    def sb(self, name, shape, dt=F32):
        return self.ctx.enter_context(self.nc.sbuf_tensor(f"{self.name}_{name}", shape, dt))

    def ps(self, name, shape, dt=F32):
        return self.ctx.enter_context(self.nc.psum_tensor(f"{self.name}_{name}", shape, dt))

    def sem(self, name):
        s = self.nc.alloc_semaphore(f"{self.name}_{name}")
        self.sems.append(s)
        return s

    def __exit__(self, *a):
        self.nc.clear_and_free_semaphores(self.sems)
        self.nc.all_engine_barrier()
        self.ctx.__exit__(*a)


class Shared:
    pass


def constants(nc, g):
    with Stage(nc, "const") as st:
        made = st.sem("made")
        with nc.Block() as block:
            @block.vector
            def _(v):
                nc.vector.memset(g.XT[D:P, :], 0.0)

            @block.gpsimd
            def _(pool):
                nc.gpsimd.memset(g.ident[:], 0.0).then_inc(made, 1)
                nc.gpsimd.memset(g.ones[:], 1.0).then_inc(made, 1)
                nc.gpsimd.memset(g.eps[:], 1e-5).then_inc(made, 1)
                pool.wait_ge(made, 3)
                nc.gpsimd.affine_select(out=g.ident[:], in_=g.ident[:], compare_op=ALU.not_equal, fill=1.0,
                                        base=0, pattern=[[-1, P]], channel_multiplier=1).then_inc(made, 1)
                pool.wait_ge(made, 4)
                nc.gpsimd.tensor_copy(g.identb[:], g.ident[:]).then_inc(made, 1)
                nc.gpsimd.iota(g.lane[:], pattern=[[0, 1]], base=0, channel_multiplier=1,
                               allow_small_or_imprecise_dtypes=True).then_inc(made, 1)
                pool.wait_ge(made, 6)


def embed(nc, g, ids, tables, W, b):
    V = [t.shape[0] for t in tables]
    EMB = tables[0].shape[1]
    KD = EMB * len(tables)
    groups = [(0, 1), (2,), (3,), (4, 5)]
    NG = len(groups)
    NI = TILES // 4
    SEL_DONE = 1 + 3 * NG + sum(len(x) == 2 for x in groups)
    with Stage(nc, "embed") as st:
        ids32 = g.XT[0:6, :].bitcast(I32)
        idsb = g.X[0:6].rearrange("p t d -> p (t d)").bitcast(BF16)[:, 0:TOKENS]
        w = st.sb("w", [D, KD])
        wq = st.sb("wq", [D, KD])
        tot = st.sb("tot", [D, 1])
        scale = st.sb("scale", [D, 1])
        scale_eps = st.sb("scale_eps", [D, 1])
        wT = st.sb("wT", [KD, D])
        eg = st.sb("eg", [P, NG, KD])
        egT = st.sb("egT", [KD, NG, P])
        F = st.sb("F", [P, NG, D])
        lane_in = st.sb("lane_in", [P, NG])
        sel = st.sb("sel", [6, NG, P], BF16)
        hot = st.sb("hot", [P, 2, NG, 512])
        bias = st.sb("bias", [P, D])
        prep = st.ps("prep", [P, 512])
        spread = [st.ps(f"spread{k}", [P, 512]) for k in range(4)]
        z = [st.ps(f"z{k}", [P, 4, D]) for k in range(2)]
        cleared, loaded, own = st.sem("cleared"), st.sem("loaded"), st.sem("vec_own")
        ids_in, ids_cast = st.sem("ids_in"), st.sem("ids_cast")
        sel_ready = st.sem("sel_ready")
        pe_prep, prep_read = st.sem("pe_prep"), st.sem("prep_read")
        abs_sum, weff = st.sem("abs_sum"), st.sem("weff")
        spread_full, hot_full, z_full, z_free = (st.sem(n) for n in ("spread_full", "hot_full", "z_full", "z_free"))
        F_ready, passed = st.sem("F_ready"), st.sem("pe_passed")
        with nc.Block() as block:
            @block.sync
            def _(sp):
                for k, t in enumerate(ids):
                    sp.dma_start(ids32[k:k + 1, :], t.rearrange("b s -> (b s)").unsqueeze(0)).then_inc(ids_in, 16)
                sp.dma_start(w[:], W).then_inc(loaded, 16)
                sp.dma_start(bias[:], b.partition_broadcast(P)).then_inc(loaded, 16)
                sp.wait_ge(cleared, 1)
                for n, grp in enumerate(groups):
                    for m, k in enumerate(grp):
                        sp.dma_start(eg[64 * m:64 * m + V[k], n, EMB * k:EMB * (k + 1)], tables[k]).then_inc(loaded, 16)

            @block.gpsimd
            def _(pool):
                nc.gpsimd.memset(eg[:], 0.0).then_inc(cleared, 1)
                nc.gpsimd.memset(sel[:], 1.0).then_inc(sel_ready, 1)
                pool.wait_ge(sel_ready, 1)
                done = 1
                for n, grp in enumerate(groups):
                    for m in range(2):
                        half = sel[:, n, 64 * m:64 * m + 64]
                        k = grp[m] if len(grp) == 2 else grp[0]
                        nc.gpsimd.affine_select(out=half, in_=half, compare_op=ALU.is_equal, fill=0.0, base=-k,
                                                pattern=[[0, 64]], channel_multiplier=1).then_inc(sel_ready, 1)
                        done += 1
                        pool.wait_ge(sel_ready, done)
                    nc.gpsimd.tensor_copy(lane_in[:, n:n + 1], g.lane[:]).then_inc(sel_ready, 1)
                    done += 1
                    pool.wait_ge(sel_ready, done)
                    if len(grp) == 2:
                        nc.gpsimd.tensor_scalar(lane_in[64:128, n:n + 1], g.lane[64:128, :], -64.0, None,
                                                ALU.add).then_inc(sel_ready, 1)
                        done += 1
                        pool.wait_ge(sel_ready, done)
                assert done == SEL_DONE

            @block.vector
            def _(v):
                link = chain(v, own)
                v.wait_ge(loaded, 16 * 8)
                nc.vector.tensor_reduce(tot[:], w[:], AX.X, ALU.add, apply_absolute_value=True).then_inc(abs_sum, 1)
                v.wait_ge(pe_prep, 1)
                link(nc.vector.tensor_scalar(scale[:], prep[0:D, 0:1], 1.0 / (D * KD), None, ALU.mult))
                link(nc.vector.tensor_scalar(scale_eps[:], scale[:], 1e-8, None, ALU.add))
                link(nc.vector.reciprocal(scale_eps[:], scale_eps[:]))
                link(nc.vector.tensor_scalar(wq[:], w[:], scale_eps[:], None, ALU.mult))
                link(nc.vector.tensor_scalar(wq[:], wq[:], 12582912.0, None, ALU.add))
                link(nc.vector.tensor_scalar(wq[:], wq[:], -12582912.0, None, ALU.add))
                link(nc.vector.tensor_scalar(wq[:], wq[:], -1.0, 1.0, ALU.max, ALU.min))
                link(nc.vector.tensor_scalar(wq[:], wq[:], scale[:], None, ALU.mult))
                link(nc.vector.tensor_tensor(wq[:], wq[:], w[:], ALU.subtract))
                nc.vector.tensor_tensor(wq[:], wq[:], w[:], ALU.add).then_inc(weff, 1)
                v.wait_ge(pe_prep, 2)
                nc.vector.tensor_copy(wT[:], prep[0:KD, 0:D]).then_inc(prep_read, 1)
                v.wait_ge(pe_prep, 3)
                nc.vector.tensor_copy(egT[:].rearrange("k n p -> k (n p)"), prep[0:KD, :]).then_inc(prep_read, 1)
                v.wait_ge(pe_prep, 4)
                nc.vector.tensor_copy(F[:].rearrange("p n d -> p (n d)"), prep[:, 0:NG * D]).then_inc(F_ready, 1)
                v.wait_ge(ids_in, 16 * len(ids))
                nc.vector.tensor_copy(idsb, ids32).then_inc(ids_cast, 1)
                v.wait_ge(sel_ready, SEL_DONE)
                v.sem_inc(z_free, 2)
                with v.Fori(0, NI // 2) as i:
                    for k in range(2):
                        for n in range(NG):
                            v.wait_ge(spread_full, (2 * i + k) * NG + n + 1)
                            if n == 0:
                                v.wait_ge(z_full, 2 * i + k + 1)
                            nc.vector.tensor_scalar(hot[:, k, n, :], spread[n][:], lane_in[:, n:n + 1], None,
                                                    ALU.is_equal).then_inc(hot_full, 1)
                        v.wait_ge(z_full, 2 * i + k + 3)
                        nc.vector.tensor_tensor(g.H[:, ds(8 * i + 4 * k, 4), :], z[k][:], bc(bias[:], 1, 4),
                                                ALU.add).then_inc(z_free, 1)
                v.wait_ge(z_free, NI + 2)

            @block.tensor
            def _(pe):
                pe.wait_ge(abs_sum, 1)
                nc.tensor.matmul(prep[0:D, 0:1], g.ones[0:D, 0:D], tot[:], start=True, stop=True).then_inc(pe_prep, 1)
                pe.wait_ge(weff, 1)
                nc.tensor.transpose(prep[0:KD, 0:D], wq[:], g.ident[0:D, 0:D]).then_inc(pe_prep, 1)
                pe.wait_ge(loaded, 16 * 8)
                pe.wait_ge(prep_read, 1)
                for n in range(NG):
                    t = nc.tensor.transpose(prep[0:KD, n * P:(n + 1) * P], eg[:, n, :], g.ident[:])
                t.then_inc(pe_prep, 1)
                pe.wait_ge(prep_read, 2)
                for n in range(NG):
                    t = nc.tensor.matmul(prep[:, n * D:(n + 1) * D], egT[:, n, :], wT[:], start=True, stop=True)
                t.then_inc(pe_prep, 1)
                pe.wait_ge(ids_cast, 1)
                pe.wait_ge(sel_ready, SEL_DONE)
                pe.wait_ge(F_ready, 1)
                pe.sem_inc(z_full, 2)
                pe.sem_inc(hot_full, NG)
                with pe.Fori(0, NI // 2) as i:
                    for k in range(2):
                        for n in range(NG):
                            wait_apart(pe, hot_full, (2 * i + k) * NG + n + 1, passed)
                            nc.tensor.matmul(spread[n][:], sel[:, n, :], idsb[:, ds((2 * i + k) * 512, 512)],
                                             start=True, stop=True).then_inc(spread_full, 1)
                        pe.wait_ge(hot_full, (2 * i + k) * NG + 2 * NG)
                        pe.wait_ge(z_free, 2 * i + k + 1)
                        for j in range(4):
                            for n in range(NG):
                                t = nc.tensor.matmul(z[k][:, j, :], hot[:, k, n, j * P:(j + 1) * P], F[:, n, :],
                                                     start=n == 0, stop=n == NG - 1)
                        t.then_inc(z_full, 1)


def layernorm(nc, g, name, src, gamma=None, beta=None, keep=None, transposed=False, add=None):
    HT = 16
    NI = TILES // (2 * HT)
    N2 = D // 2
    with Stage(nc, name) as st:
        xn = st.sb("xn", [P, 2, HT, D])
        stats = st.sb("stats", [P, TILES, 6])
        mean, var, std, rstd, gap = (st.sb(n, [P, TILES]) for n in ("mean", "var", "std", "rstd", "gap"))
        if gamma is not None:
            gam, bet = st.sb("gamma", [P, D]), st.sb("beta", [P, D])
        if transposed:
            pt = [st.ps(f"pt{k}", [P, HT // 2 * P]) for k in range(2)]
        params, own = st.sem("params"), st.sem("vec_own")
        var_ready, std_ready = st.sem("var_ready"), st.sem("std_ready")
        normed, turned, evacuated, kept = (st.sem(n) for n in ("normed", "turned", "evacuated", "kept"))
        copies = keep is not None and transposed
        with nc.Block() as block:
            if gamma is not None:
                @block.sync
                def _(sp):
                    sp.dma_start(gam[:], gamma.partition_broadcast(P)).then_inc(params, 16)
                    sp.dma_start(bet[:], beta.partition_broadcast(P)).then_inc(params, 16)

            @block.vector
            def _(v):
                vec = nc.vector
                link = chain(v, own)
                for t in range(TILES):
                    m = vec.bn_stats(stats[:, t, :], src[:, t, :])
                link(m)
                even, odd = stats[:, :, 1], stats[:, :, 4]
                vec.tensor_tensor(mean[:], even, odd, ALU.add)
                vec.tensor_tensor(var[:], stats[:, :, 2], stats[:, :, 5], ALU.add)
                link(vec.tensor_tensor(gap[:], even, odd, ALU.subtract))
                vec.tensor_scalar(mean[:], mean[:], 0.5, None, ALU.mult)
                link(vec.tensor_tensor(gap[:], gap[:], gap[:], ALU.mult))
                vec.scalar_tensor_tensor(var[:], gap[:], N2 / 2, var[:], ALU.mult, ALU.add).then_inc(var_ready, 1)
                v.wait_ge(std_ready, 1)
                link(vec.reciprocal(rstd[:], std[:]))
                if gamma is not None:
                    v.wait_ge(params, 32)
                base = link.count[0]
                steps = [lambda to, x, s: vec.tensor_tensor(to, x, bc(mean[:, s], 2, D), ALU.subtract),
                         lambda to, x, s: vec.tensor_tensor(to, x, bc(rstd[:, s], 2, D), ALU.mult)]
                if gamma is not None:
                    steps += [lambda to, x, s: vec.tensor_tensor(to, x, bc(gam[:], 1, HT), ALU.mult),
                              lambda to, x, s: vec.tensor_tensor(to, x, bc(bet[:], 1, HT), ALU.add)]
                if add is not None:
                    steps += [lambda to, x, s: vec.tensor_tensor(to, x, add[:, s, :], ALU.add)]
                to_keep = None if transposed else g.H if add is not None else keep
                with v.Fori(0, NI) as i:
                    for n, step in enumerate(steps):
                        last = n == len(steps) - 1
                        for k in range(2):
                            s = ds((i * 2 + k) * HT, HT)
                            if n == 0:
                                if transposed:
                                    v.wait_ge(turned, 2 * i + k + 1)
                                if copies:
                                    v.wait_ge(kept, 2 * i + k + 1)
                            else:
                                v.wait_ge(own, base + i * 2 * (len(steps) - 1) + 2 * (n - 1) + k + 1)
                            to = to_keep[:, s, :] if last and to_keep is not None else xn[:, k]
                            m = step(to, src[:, s, :] if n == 0 else xn[:, k], s)
                            m.then_inc(normed if last else own, 1)
                    if not transposed:
                        v.wait_ge(normed, 2 * i + 2)

            @block.scalar
            def _(act):
                act.wait_ge(var_ready, 1)
                nc.scalar.activation(std[:], var[:], ACT.Sqrt, bias=g.eps[:], scale=1.0 / D).then_inc(std_ready, 1)
                if transposed:
                    act.sem_inc(evacuated, 4)
                    if copies:
                        act.sem_inc(kept, 2)
                    with act.Fori(0, NI) as i:
                        for k in range(2):
                            if copies:
                                act.wait_ge(normed, 2 * i + k + 1)
                                nc.scalar.copy(keep[:, ds((i * 2 + k) * HT, HT), :], xn[:, k]).then_inc(kept, 1)
                            act.wait_ge(turned, 2 * i + k + 3)
                            xt = g.XT[0:D, ds((i * 2 + k) * HT * P, HT * P)].rearrange("d (m two q) -> d m two q", two=2, q=P)
                            for odd in range(2):
                                nc.scalar.copy(xt[:, :, odd, :], pt[k][D * odd:D * odd + D, :].rearrange("d (m q) -> d m q", q=P)).then_inc(evacuated, 1)

            if transposed:
                @block.tensor
                def _(pe):
                    pe.sem_inc(turned, 2)
                    with pe.Fori(0, NI) as i:
                        for k in range(2):
                            pe.wait_ge(normed, 2 * i + k + 1)
                            pe.wait_ge(evacuated, 4 * i + 2 * k + 2)
                            for m in range(HT // 2):
                                t = nc.tensor.transpose(pt[k][:, m * P:(m + 1) * P],
                                                        xn[:, k, 2 * m:2 * m + 2, :].rearrange("p m d -> p (m d)"), g.ident[:])
                            t.then_inc(turned, 1)



def top2_steps(nc, v, link, st, L, G, E, hot, tmp):
    n, N = L.shape[0], L.shape[1]
    rev = st.sb("rev", [n, E])
    v1, v2, r, w1, w2 = (st.sb(x, [n, N]) for x in ("v1", "v2", "r", "w1", "w2"))
    made = st.sem("rev_made")
    diff_ready, exp_ready = st.sem("top2_diff"), st.sem("top2_exp")

    def pool_part(pool):
        nc.gpsimd.iota(rev[:], pattern=[[-1, E]], base=E, channel_multiplier=0,
                       allow_small_or_imprecise_dtypes=True).then_inc(made, 1)

    def act_part(act):
        act.wait_ge(diff_ready, 1)
        nc.scalar.activation(w2[:], v2[:], ACT.Exp).then_inc(exp_ready, 1)

    def one_hot(best):
        link(nc.vector.tensor_reduce(best[:], L, AX.X, ALU.max))
        link(nc.vector.tensor_tensor(hot, L, bc(best[:], 2, E), ALU.is_equal))
        link(nc.vector.tensor_tensor(tmp, hot, bc(rev[:], 1, N), ALU.mult))
        link(nc.vector.tensor_reduce(r[:], tmp, AX.X, ALU.max))
        link(nc.vector.tensor_tensor(hot, bc(rev[:], 1, N), bc(r[:], 2, E), ALU.is_equal))

    def vector_part():
        v.wait_ge(made, 1)
        one_hot(v1)
        link(nc.vector.tensor_copy(G, hot))
        link(nc.vector.scalar_tensor_tensor(L, hot, -3e38, L, ALU.mult, ALU.add))
        one_hot(v2)
        nc.vector.tensor_tensor(v2[:], v2[:], v1[:], ALU.subtract).then_inc(diff_ready, 1)
        v.wait_ge(exp_ready, 1)
        link(nc.vector.tensor_scalar(w1[:], w2[:], 1.0, None, ALU.add))
        link(nc.vector.reciprocal(w1[:], w1[:]))
        link(nc.vector.tensor_tensor(w2[:], w2[:], w1[:], ALU.mult))
        link(nc.vector.tensor_tensor(G, G, bc(w1[:], 2, E), ALU.mult))
        link(nc.vector.tensor_tensor(hot, hot, bc(w2[:], 2, E), ALU.mult))
        link(nc.vector.tensor_tensor(G, G, hot, ALU.add))

    return vector_part, pool_part, act_part


def route(nc, g, name, Wr, br, E, probs=False):
    with Stage(nc, name) as st:
        lg, gt = st.sb("L", [P, TILES, E]), st.sb("G", [P, TILES, E])
        L, G = lg[:], gt[:]
        w = st.sb("w", [P, E])
        bias = st.sb("bias", [P, E])
        banks = max(1, TILES * E // 512)
        step = TILES // banks
        pl = st.ps("logits", [P, TILES, E])
        loaded, own, bank_full, cleared = st.sem("loaded"), st.sem("vec_own"), st.sem("bank_full"), st.sem("cleared")
        if probs:
            rsum, mx = st.sb("rsum", [P, TILES]), st.sb("mx", [P, TILES])
            shifted, exped = st.sem("shifted"), st.sem("exped")
        hot, tmp = g.X[:, :, 0:E], g.X[:, :, E:2 * E]
        gates = GateSplit(nc, g, st, E, tmp)
        with nc.Block() as block:
            parts = {}

            @block.sync
            def _(sp):
                sp.dma_start(w[0:D, :], Wr).then_inc(loaded, 16)
                sp.dma_start(bias[:], br.partition_broadcast(P)).then_inc(loaded, 16)

            @block.tensor
            def _(pe):
                pe.wait_ge(loaded, 32)
                pe.wait_ge(cleared, 1)
                for t in range(TILES):
                    m = nc.tensor.matmul(pl[:, t, :], g.XT[:, t * P:(t + 1) * P], w[:], start=True, stop=True)
                    if (t + 1) % step == 0:
                        m.then_inc(bank_full, 1)
                gates.tensor(pe)

            @block.vector
            def _(v):
                link = chain(v, own)
                nc.vector.memset(w[D:P, :], 0.0).then_inc(cleared, 1)
                v.wait_ge(loaded, 32)
                for n in range(banks):
                    v.wait_ge(bank_full, n + 1)
                    s = slice(n * step, (n + 1) * step)
                    link(nc.vector.tensor_tensor(L[:, s], pl[:, s, :], bc(bias[:], 1, step), ALU.add))
                if probs:
                    link(nc.vector.tensor_reduce(mx[:], L, AX.X, ALU.max))
                    nc.vector.tensor_tensor(L, L, bc(mx[:], 2, E), ALU.subtract).then_inc(shifted, 1)
                    v.wait_ge(exped, 1)
                    link(nc.vector.reduce_sum(rsum[:], L, AX.X))
                    link(nc.vector.reciprocal(rsum[:], rsum[:]))
                    link(nc.vector.tensor_tensor(L, L, bc(rsum[:], 2, E), ALU.mult))
                    parts["pool"] = ratio_steps(nc, v, link, st, L, G, E, hot, tmp)
                else:
                    vec, parts["pool"], parts["act"] = top2_steps(nc, v, link, st, L, G, E, hot, tmp)
                    vec()
                gates.vector(link, G)

            @block.gpsimd
            def _(pool):
                parts["pool"](pool)
                gates.gpsimd()

            @block.scalar
            def _(act):
                if probs:
                    act.wait_ge(shifted, 1)
                    nc.scalar.activation(L, L, ACT.Exp).then_inc(exped, 1)
                else:
                    parts["act"](act)
                gates.scalar(act)


class GateSplit:

    def __init__(self, nc, g, st, E, scratch):
        self.nc, self.g, self.E = nc, g, E
        self.g3 = st.sb("g3", [P, TILES, 3, E], BF16)
        self.rest = scratch
        self.pt = [st.ps(f"gt{k}", [3 * E, 8 * P], BF16) for k in range(2)]
        self.split, self.turned, self.moved, self.zeroed = (
            st.sem(n) for n in ("gates_split", "gates_turned", "gates_moved", "GT_zeroed"))

    def gpsimd(self):
        self.nc.gpsimd.memset(self.g.GT[:].bitcast(F32), 0.0).then_inc(self.zeroed, 1)

    def vector(self, link, G):
        v = self.nc.vector
        link(v.tensor_copy(self.g3[:, :, 0, :], G))
        link(v.tensor_tensor(self.rest, G, self.g3[:, :, 0, :], ALU.subtract))
        link(v.tensor_copy(self.g3[:, :, 1, :], self.rest))
        link(v.tensor_tensor(self.rest, self.rest, self.g3[:, :, 1, :], ALU.subtract))
        v.tensor_copy(self.g3[:, :, 2, :], self.rest).then_inc(self.split, 1)

    def tensor(self, pe):
        pe.wait_ge(self.split, 1)
        for c in range(TILES // 8):
            if c >= 2:
                pe.wait_ge(self.moved, c - 1)
            for m in range(8):
                t = self.nc.tensor.transpose(self.pt[c % 2][:, m * P:(m + 1) * P],
                                             self.g3[:, 8 * c + m].rearrange("p s e -> p (s e)"), self.g.identb[:])
            t.then_inc(self.turned, 1)

    def scalar(self, act):
        act.wait_ge(self.zeroed, 1)
        for c in range(TILES // 8):
            act.wait_ge(self.turned, c + 1)
            self.nc.scalar.copy(self.g.GT[0:3 * self.E, c * 8 * P:(c + 1) * 8 * P], self.pt[c % 2][:]).then_inc(self.moved, 1)


def ratio_steps(nc, v, link, st, L, G, E, hot, tmp):
    N = L.shape[1]
    rev = st.sb("rev", [P, E])
    best, r, total = (st.sb(x, [P, N]) for x in ("best", "r", "total"))
    made = st.sem("rev_made")
    v.wait_ge(made, 1)
    for turn in range(2):
        link(nc.vector.tensor_reduce(best[:], L, AX.X, ALU.max))
        link(nc.vector.tensor_tensor(hot, L, bc(best[:], 2, E), ALU.is_equal))
        link(nc.vector.tensor_tensor(tmp, hot, bc(rev[:], 1, N), ALU.mult))
        link(nc.vector.tensor_reduce(r[:], tmp, AX.X, ALU.max))
        link(nc.vector.tensor_tensor(hot, bc(rev[:], 1, N), bc(r[:], 2, E), ALU.is_equal))
        if turn == 0:
            link(nc.vector.tensor_tensor(G, hot, bc(best[:], 2, E), ALU.mult))
            link(nc.vector.tensor_copy(total[:], best[:]))
            link(nc.vector.scalar_tensor_tensor(L, hot, -4.0, L, ALU.mult, ALU.add))
        else:
            link(nc.vector.tensor_tensor(hot, hot, bc(best[:], 2, E), ALU.mult))
            link(nc.vector.tensor_tensor(G, G, hot, ALU.add))
            link(nc.vector.tensor_tensor(total[:], total[:], best[:], ALU.add))
    link(nc.vector.reciprocal(total[:], total[:]))
    link(nc.vector.tensor_tensor(G, G, bc(total[:], 2, E), ALU.mult))

    def pool_part(pool):
        nc.gpsimd.iota(rev[:], pattern=[[-1, E]], base=E, channel_multiplier=0,
                       allow_small_or_imprecise_dtypes=True).then_inc(made, 1)

    return pool_part


def experts(nc, g, name, W1, W2, b1=None, b2=None, Wg=None, target=None):
    E, _, F = W1.shape
    U = 512
    UT = U // P
    NI = TOKENS // U
    SLOTS = 2
    with Stage(nc, name) as st:
        XTb = g.XT[:].bitcast(BF16)
        lhs = [[st.sb(f"w{n}_{part}", [P, E, F], BF16) for part in ("hh", "mm", "hl")] for n in range(1 + (Wg is not None))]
        if Wg is not None:
            room = g.X[:].rearrange("p t d -> p (t d)")
            raw, left = (room[:, n * E * F:(n + 1) * E * F].rearrange("p (e f) -> p e f", e=E) for n in range(2))
            raw2 = room[:, 2 * E * F:3 * E * F].rearrange("p (e f) -> p e f", e=E)
        else:
            raw, left = st.sb("raw", [P, E, F])[:], st.sb("left", [P, E, F])[:]
            raw2 = None
        raws = [raw] if Wg is None else [raw, raw2]
        zero = st.sb("zero", [P, 1])
        x_high, x_mid, x_left = st.sb("x_high", [D, U], BF16), st.sb("x_mid", [D, U], BF16), st.sb("x_left", [D, U])
        w2 = st.sb("w2", [F, E, D])
        if Wg is None:
            b1s, b2f, b2s, rest = st.sb("b1", [F, E]), st.sb("b2f", [P, D]), st.sb("b2", [P, D], BF16), st.sb("b2rest", [P, D])
            b2lo = [st.sb(f"b2lo{n}", [P, D], BF16) for n in range(2)]
        act_out = st.sb("act_out", [F, SLOTS, U])
        gate = st.sb("gate", [F, SLOTS, U])[:] if Wg is None else room[:, 3 * E * F:3 * E * F + SLOTS * U].rearrange(
            "p (s u) -> p s u", s=SLOTS)
        hid = st.sb("hid", [F, SLOTS, U])
        pick = st.sb("pick", [P, E, P], BF16)
        yT = st.sb("yT", [D, U])
        hp = [st.ps(f"hp{s}", [F, U]) for s in range(SLOTS)]
        h2 = [st.ps(f"h2{s}", [F, U]) for s in range(SLOTS)] if Wg is not None else None
        gp = [st.ps(f"gp{s}", [F, U]) for s in range(SLOTS)]
        yp = st.ps("yp", [D, U])
        yt = st.ps("yt", [P, UT, D])
        loaded, cleared, own = st.sem("loaded"), st.sem("cleared"), st.sem("vec_own")
        picked, passed = st.sem("picked"), st.sem("pe_passed")
        gp_full, h2_full, hp_full, gate_ready, product_ready, act_done, hid_full, hid_used = (
            st.sem(n) for n in ("gp_full", "h2_full", "hp_full", "gate_ready", "product_ready", "act_done",
                                "hid_full", "hid_used"))
        y_full, y_moved, y_turned, y_added = (st.sem(n) for n in ("y_full", "y_moved", "y_turned", "y_added"))
        b2_ready = st.sem("b2_ready")
        w_split, high_ready, left_ready, mid_ready, x_split = (
            st.sem(n) for n in ("w_split", "high_ready", "left_ready", "mid_ready", "x_split"))
        AHEAD = 2

        def pipeline(eng, turn):
            turn(0, first=True)
            with eng.Fori(0, NI - 2) as i:
                turn(i + 1)
            turn(NI - 1, last=True)

        LOADS = 7 if Wg is None else 5
        CLEARED = 1 if Wg is not None else 2
        with nc.Block() as block:
            @block.sync
            def _(sp):
                for to, W in zip(raws, (W1, Wg)):
                    for half in range(2):
                        sp.dma_start(to[D * half:D * half + D], W.rearrange("e d f -> d e f")).then_inc(loaded, 16)
                sp.dma_start(w2[:], W2.rearrange("e f d -> f e d")).then_inc(loaded, 16)
                if Wg is None:
                    with nc.allow_non_contiguous_dma(reason="small bias, turned"):
                        sp.dma_start(b1s[:], b1.rearrange("e f -> f e")).then_inc(loaded, 16)
                    sp.wait_ge(cleared, CLEARED)
                    for n in range(3):
                        sp.dma_start(b2f[n * E:(n + 1) * E, :], b2).then_inc(loaded, 16)

            @block.gpsimd
            def _(pool):
                nc.gpsimd.memset(pick[:].rearrange("p e q -> p (e q)").bitcast(F32), 0.0).then_inc(cleared, 1)
                pool.wait_ge(cleared, CLEARED)
                for n in range(3):
                    nc.gpsimd.affine_select(out=pick[:], in_=pick[:], compare_op=ALU.not_equal, fill=1.0, base=-n * E,
                                            pattern=[[-1, E], [0, P]], channel_multiplier=1).then_inc(picked, 1)
                    pool.wait_ge(picked, n + 1)

            @block.tensor
            def _(pe):
                pe.wait_ge(loaded, 16 * LOADS)
                pe.wait_ge(picked, 3)
                pe.wait_ge(w_split, len(lhs))
                if Wg is None:
                    pe.wait_ge(b2_ready, 3)

                pe.sem_inc(y_turned, 1)

                def hidden(i, e):
                    s = e % SLOTS
                    if e == 0:
                        wait_apart(pe, x_split, i + 1, passed)
                    wait_apart(pe, act_done, i * E + e + 1, passed)
                    if Wg is not None:
                        wait_apart(pe, product_ready, i * E + e + 1, passed)
                    nc.tensor.matmul(gp[s][:], pick[:, e, :], g.GT[:, ds(i * U, U)], start=True, stop=True).then_inc(gp_full, 1)
                    hm, lh = XTb[:, ds(i * 2 * U, U)], XTb[:, ds(i * 2 * U + U, U)]
                    for bank, w, full in list(zip((hp, h2), lhs, (hp_full, h2_full)))[::-1]:
                        for n, x in enumerate((hm, hm, lh)):
                            m = nc.tensor.matmul(bank[s][:], w[n][:, e, :], x, start=n == 0, stop=n == 2)
                        m.then_inc(full, 1)

                def turn_back(i):
                    wait_apart(pe, y_moved, i + 2, passed)
                    wait_apart(pe, y_added, i + 1, passed)
                    for j in range(UT):
                        m = nc.tensor.transpose(yt[:, j, :], yT[:, j * P:(j + 1) * P], g.ident[0:D, 0:D])
                    m.then_inc(y_turned, 1)

                def turn(i, first=False, last=False):
                    for e in range(E):
                        if e + AHEAD < E:
                            hidden(i, e + AHEAD)
                        elif not last:
                            hidden(i + 1, e + AHEAD - E)
                        if e == 0:
                            wait_apart(pe, y_moved, i + 1, passed)
                            if Wg is None:
                                for n, b in enumerate((b2s, *b2lo)):
                                    nc.tensor.matmul(yp[:], b[:], g.GT[:, ds(i * U, U)], start=n == 0, stop=False)
                        wait_apart(pe, hid_full, i * E + e + 1 + SLOTS, passed)
                        m = nc.tensor.matmul(yp[:], w2[:, e, :], hid[:, e % SLOTS, :],
                                             start=e == 0 and Wg is not None, stop=e == E - 1)
                        m.then_inc(hid_used, 1)
                        if e == 1 and not first:
                            turn_back(i - 1)

                for e in range(AHEAD):
                    hidden(0, e)
                pipeline(pe, turn)
                turn_back(NI - 1)

            @block.scalar
            def _(act):
                act.wait_ge(loaded, 16 * LOADS)
                act.sem_inc(y_moved, 1)
                act.sem_inc(act_done, SLOTS)

                def high(c):
                    if not (isinstance(c, int) and c == 0):
                        act.wait_ge(x_split, c)
                    nc.scalar.copy(x_high[:], g.XT[0:D, ds(c * U, U)]).then_inc(high_ready, 1)

                def mid(c):
                    act.wait_ge(left_ready, c + 1)
                    nc.scalar.copy(x_mid[:], x_left[:]).then_inc(mid_ready, 1)

                def move_y(i):
                    act.wait_ge(hid_used, (i + 1) * E + SLOTS)
                    act.wait_ge(y_turned, i + 1)
                    nc.scalar.copy(yT[:], yp[:]).then_inc(y_moved, 1)

                def turn(i, first=False, last=False):
                    for e in range(E):
                        s = e % SLOTS
                        act.wait_ge(gp_full, i * E + e + 1)
                        act.wait_ge(hid_full, i * E + e + 1)
                        nc.scalar.copy(gate[:, s], gp[s][:]).then_inc(gate_ready, 1)
                        act.wait_ge(hp_full, i * E + e + 1)
                        if Wg is None:
                            nc.scalar.activation(act_out[:, s], hp[s][:], ACT.Gelu, bias=b1s[:, e:e + 1]).then_inc(act_done, 1)
                        else:
                            nc.scalar.activation(act_out[:, s], hp[s][:], ACT.Silu).then_inc(act_done, 1)
                        if e == 0:
                            if not first:
                                move_y(i - 1)
                            if not last:
                                high(i + 1)
                        if e == 1 and not last:
                            mid(i + 1)

                high(0)
                mid(0)
                pipeline(act, turn)
                move_y(NI - 1)

            @block.vector
            def _(v):
                if Wg is None:
                    nc.vector.memset(b2f[:], 0.0).then_inc(cleared, 1)
                v.sem_inc(hid_full, SLOTS)
                v.sem_inc(product_ready, SLOTS)
                v.sem_inc(hid_used, SLOTS)
                v.sem_inc(y_added, 1)
                v.wait_ge(loaded, 16 * LOADS)
                link = chain(v, own)
                link(nc.vector.memset(zero[:], 0.0))

                def remainder(c):
                    v.wait_ge(high_ready, c + 1)
                    nc.vector.tensor_tensor(x_left[:], g.XT[0:D, ds(c * U, U)], x_high[:], ALU.subtract).then_inc(left_ready, 1)

                def place(c):
                    v.wait_ge(mid_ready, c + 1)
                    hm, lh = XTb[:, ds(c * 2 * U, U)], XTb[:, ds(c * 2 * U + U, U)]
                    nc.vector.tensor_tensor(lh[0:D], x_left[:], x_mid[:], ALU.subtract)
                    nc.vector.tensor_copy(hm[0:D], x_high[:])
                    nc.vector.tensor_copy(hm[D:P], x_mid[:])
                    nc.vector.tensor_copy(lh[D:P], x_high[:]).then_inc(x_split, 1)

                remainder(0)
                place(0)
                for n, (raw_w, (hh, mm, hl)) in enumerate(zip(raws, lhs)):
                    link(nc.vector.tensor_copy(hh[:], raw_w))
                    nc.vector.tensor_copy(hl[0:D], hh[0:D])
                    link(nc.vector.tensor_tensor(left, raw_w, hh[:], ALU.subtract))
                    link(nc.vector.tensor_copy(mm[:], left))
                    nc.vector.tensor_tensor(hl[D:P], left[D:P], mm[D:P], ALU.subtract).then_inc(w_split, 1)
                    v.wait_ge(w_split, n + 1)
                if Wg is None:
                    nc.vector.tensor_copy(b2s[:], b2f[:]).then_inc(b2_ready, 1)
                    v.wait_ge(b2_ready, 1)
                    link(nc.vector.tensor_tensor(rest[:], b2f[:], b2s[:], ALU.subtract))
                    nc.vector.tensor_copy(b2lo[0][:], rest[:]).then_inc(b2_ready, 1)
                    v.wait_ge(b2_ready, 2)
                    link(nc.vector.tensor_tensor(rest[:], rest[:], b2lo[0][:], ALU.subtract))
                    nc.vector.tensor_copy(b2lo[1][:], rest[:]).then_inc(b2_ready, 1)
                def add(i):
                    v.wait_ge(y_turned, i + 2)
                    h = target[:, ds(i * UT, UT), :]
                    nc.vector.tensor_tensor(h, h, yt[:], ALU.add).then_inc(y_added, 1)
                    nc.vector.tensor_copy(g.XT[D:P, ds(i * U, U)], bc(zero[D:P, 0], 1, U))

                def turn(i, first=False, last=False):
                    for e in range(E):
                        s = e % SLOTS
                        if Wg is not None:
                            v.wait_ge(gate_ready, i * E + e + 1)
                            v.wait_ge(h2_full, i * E + e + 1)
                            nc.vector.tensor_tensor(gate[:, s], gate[:, s], h2[s][:], ALU.mult).then_inc(product_ready, 1)
                            v.wait_ge(product_ready, i * E + e + 1 + SLOTS)
                        v.wait_ge(act_done, i * E + e + 1 + SLOTS)
                        v.wait_ge(hid_used, i * E + e + 1)
                        nc.vector.tensor_tensor(hid[:, s], act_out[:, s], gate[:, s], ALU.mult).then_inc(hid_full, 1)
                        if e == 0 and not last:
                            remainder(i + 1)
                        if e == 2 and not first:
                            add(i - 1)
                        if e == 2 and not last:
                            place(i + 1)

                pipeline(v, turn)
                add(NI - 1)


def allocate(nc, ctx):
    g = Shared()

    def sb(name, shape, dt=F32):
        return ctx.enter_context(nc.sbuf_tensor(name, shape, dt))

    g.H = sb("H", [P, TILES, D])
    g.X = sb("X", [P, TILES, D])
    g.XT = sb("XT", [P, TOKENS])
    g.GT = sb("GT", [P, TOKENS], BF16)
    g.ident, g.ones = sb("ident", [P, P]), sb("ones", [P, P])
    g.identb = sb("identb", [P, P], BF16)
    g.eps, g.lane = sb("eps", [P, 1]), sb("lane", [P, 1])
    return g


def store(nc, g, out):
    with Stage(nc, "store") as st:
        stored = st.sem("stored")
        o = out.rearrange("b (j p) d -> p (b j) d", p=P)
        with nc.Block() as block:
            @block.sync
            def _(sp):
                for q in range(4):
                    t = slice(q * TILES // 4, (q + 1) * TILES // 4)
                    sp.dma_start(o[:, t, :], g.H[:, t, :]).then_inc(stored, 16)
                sp.wait_ge(stored, 64)


def attn0(nc, g, I):
    layernorm(nc, g, "ln_a0", g.H, keep=g.X, transposed=True)
    scale = D ** -0.5
    with Stage(nc, "attn0") as st:
        wq, wk = st.sb("wq", [D, D]), st.sb("wk", [D, D])
        M = st.sb("M", [P, D])
        tT = st.sb("tT", [P, 2, S])
        prob = st.sb("prob", [P, 2, TPB, S])
        probT = st.sb("probT", [P, 2, TPB, S])
        mx, nm, rs, rr = (st.sb(n, [P, 2, TPB]) for n in ("mx", "nm", "rs", "rr"))
        tp = [st.ps(f"tp{k}", [D, 512]) for k in range(2)]
        sp_ = [st.ps(f"sp{k}", [P, TPB, S]) for k in range(2)]
        pt = [st.ps(f"pt{k}", [P, TPB, S]) for k in range(2)]
        op = [st.ps(f"op{k}", [P, 512]) for k in range(2)]
        names = ("loaded", "cleared", "passed", "M_made", "M_ready", "t_full", "t_moved", "s_full", "max_ready",
                 "prob_ready", "turned", "probT_ready", "o_full", "o_added", "vec_own")
        (loaded, cleared, passed, M_made, M_ready, t_full, t_moved, s_full, max_ready,
         prob_ready, turned, probT_ready, o_full, o_added, own) = (st.sem(n) for n in names)
        with nc.Block() as block:
            @block.sync
            def _(sp):
                sp.dma_start(wq[:], I["L0_attn_Wq"]).then_inc(loaded, 16)
                sp.dma_start(wk[:], I["L0_attn_Wk"]).then_inc(loaded, 16)

            @block.tensor
            def _(pe):
                pe.wait_ge(loaded, 32)
                nc.tensor.matmul(tp[0][:, 0:D], wq[:], wk[:], start=True, stop=True).then_inc(M_made, 1)
                pe.wait_ge(M_ready, 1)
                pe.wait_ge(cleared, 2)
                with pe.Fori(0, B // 2) as i:
                    for k in range(2):
                        x = g.XT[:, ds((2 * i + k) * S, S)]
                        wait_apart(pe, t_moved, 2 * i + k + 1, passed)
                        nc.tensor.matmul(tp[k][:, 0:S], M[:], x, start=True, stop=True).then_inc(t_full, 1)
                    for k in range(2):
                        x = g.XT[:, ds((2 * i + k) * S, S)]
                        pe.wait_ge(prob_ready, 2 * (2 * i + k + 1))
                        wait_apart(pe, t_moved, 2 * i + k + 3, passed)
                        for a in range(TPB):
                            m = nc.tensor.matmul(sp_[k][:, a, :], tT[:, k, a * P:(a + 1) * P], x, start=True, stop=True)
                        m.then_inc(s_full, 1)
                    for k in range(2):
                        pe.wait_ge(probT_ready, 2 * i + k + 1)
                        pe.wait_ge(prob_ready, 2 * (2 * i + k + 1) + 4)
                        for j in range(TPB):
                            for a in range(TPB):
                                m = nc.tensor.transpose(pt[k][:, j, a * P:(a + 1) * P],
                                                        prob[:, k, a, j * P:(j + 1) * P], g.ident[:])
                        m.then_inc(turned, 1)
                    for k in range(2):
                        pe.wait_ge(o_added, 2 * (2 * i + k + 1))
                        wait_apart(pe, probT_ready, 2 * i + k + 3, passed)
                        for a in range(TPB):
                            for j in range(TPB):
                                m = nc.tensor.matmul(op[k][:, a * D:(a + 1) * D], probT[:, k, j, a * P:(a + 1) * P],
                                                     g.X[:, (2 * i + k) * TPB + j, :], start=j == 0, stop=j == TPB - 1)
                        m.then_inc(o_full, 1)

            @block.scalar
            def _(act):
                act.sem_inc(t_moved, 2)
                act.sem_inc(prob_ready, 4)
                act.sem_inc(probT_ready, 2)
                with act.Fori(0, B // 2) as i:
                    for k in range(2):
                        act.wait_ge(t_full, 2 * i + k + 1)
                        nc.scalar.copy(tT[0:D, k, :], tp[k][:, 0:S]).then_inc(t_moved, 1)
                    for k in range(2):
                        act.wait_ge(max_ready, 2 * i + k + 1)
                        act.wait_ge(turned, 2 * i + k + 1)
                        for a in range(TPB):
                            nc.scalar.activation(prob[:, k, a, :], sp_[k][:, a, :], ACT.Exp, bias=nm[:, k, a:a + 1],
                                                 scale=scale, accum_out=rs[:, k, a:a + 1]).then_inc(prob_ready, 1)
                    for k in range(2):
                        act.wait_ge(turned, 2 * i + k + 3)
                        nc.scalar.copy(probT[:, k], pt[k][:]).then_inc(probT_ready, 1)

            @block.vector
            def _(v):
                nc.vector.memset(M[D:P], 0.0).then_inc(cleared, 1)
                nc.vector.memset(tT[D:P], 0.0).then_inc(cleared, 1)
                v.sem_inc(turned, 2)
                v.sem_inc(o_added, 4)
                v.wait_ge(M_made, 1)
                nc.vector.tensor_copy(M[0:D, :], tp[0][:, 0:D]).then_inc(M_ready, 1)
                with v.Fori(0, B // 2) as i:
                    link = chain(v, own, i, 4)
                    for k in range(2):
                        v.wait_ge(s_full, 2 * i + k + 1)
                        link(nc.vector.tensor_reduce(mx[:, k], sp_[k][:], AX.X, ALU.max))
                        nc.vector.tensor_scalar(nm[:, k], mx[:, k], -scale, None, ALU.mult).then_inc(max_ready, 1)
                    for k in range(2):
                        v.wait_ge(o_full, 2 * i + k + 1)
                        link(nc.vector.reciprocal(rr[:, k], rs[:, k]))
                        for a in range(TPB):
                            h = g.H[:, (2 * i + k) * TPB + a, :]
                            nc.vector.scalar_tensor_tensor(h, op[k][:, a * D:(a + 1) * D], rr[:, k, a:a + 1], h,
                                                           ALU.mult, ALU.add).then_inc(o_added, 1)
                    assert link.count[0] == 4


def attn2(nc, g, I):
    layernorm(nc, g, "ln_a2", g.H, transposed=True)
    HEADS = 8
    HP = HEADS // 2
    scale = float((D / HEADS) ** -0.5)
    NSTEP = HP * TPB
    NS = 4
    with Stage(nc, "attn2") as st:
        room = g.X[0:D].rearrange("p t d -> p (t d)").rearrange("p (n c) -> p n c", c=HEADS * D)
        W = {w: room[:, n, :] for n, w in enumerate(("WQ", "WK", "WV"))}
        wT = {w: room[:, 3 + n, :].rearrange("p (h d) -> p h d", d=D) for n, w in enumerate(("WQ", "WK", "WV"))}
        wout = room[:, 6, :].rearrange("p (h d) -> p h d", d=D)
        A, Bm = st.sb("A", [P, HEADS * D]), st.sb("B", [P, HEADS * D])
        bout = st.sb("bout", [D, 1])
        xs = st.sb("xs", [P, 2, S])
        xlow = st.sb("xlow", [P, 2, S])
        tT = st.sb("tT", [P, 2, HP, S])
        xB = st.sb("xB", [P, 2, TPB, HEADS * D])
        prob = st.sb("prob", [P, 2, 2, S])
        probT = st.sb("probT", [P, 2, 2, TPB, S])
        mx, nm, rs, rr = (st.sb(n, [P, 4, 2]) for n in ("mx", "nm", "rs", "rr"))
        oT = st.sb("oT", [D, S])
        sc = [st.ps(f"sc{k}", [P, 2, S]) for k in range(NS)]
        pt = [st.ps(f"pt{k}", [P, 2, TPB, P]) for k in range(2)]
        tx = st.ps("tx", [P, 512])
        otb = st.ps("ot", [P, 512])
        ot, ott = otb[0:D, 0:S], otb[:, S:S + TPB * D].rearrange("p (a d) -> p a d", d=D)
        names = ("loaded", "cleared", "passed", "w_turned", "w_moved", "ab_made", "ab_moved", "tx_full",
                 "tx_moved", "s_full", "max_ready", "exp_done", "prob_ready", "turned", "probT_ready", "pv_done",
                 "oT_ready", "o_turned", "o_added", "vec_own")
        (loaded, cleared, passed, w_turned, w_moved, ab_made, ab_moved, tx_full,
         tx_moved, s_full, max_ready, exp_done, prob_ready, turned, probT_ready, pv_done,
         oT_ready, o_turned, o_added, own) = (st.sem(n) for n in names)
        x_staged = [st.sem(f"x_staged{k}") for k in range(2)]
        with nc.Block() as block:
            @block.sync
            def _(sp):
                for n in ("WQ", "WK", "WV"):
                    sp.dma_start(W[n], I["L2_attn_" + n]).then_inc(loaded, 16)
                sp.dma_start(wout, I["L2_attn_Wout"].rearrange("(h c) o -> c h o", c=D)).then_inc(loaded, 16)
                sp.dma_start(bout[:], I["L2_attn_bout"].unsqueeze(1)).then_inc(loaded, 16)
                sp.wait_ge(cleared, 2)
                with sp.Fori(0, B // 2) as i:
                    for k in range(2):
                        x = g.XT[0:D, ds((2 * i + k) * S, S)]
                        sp.wait_ge(s_full, NSTEP * (2 * i + k + 1))
                        sp.dma_start(xs[0:D, k, :], x).then_inc(x_staged[k], 16)
                        sp.dma_start(xlow[D:P, k, :], x).then_inc(x_staged[k], 16)

            @block.tensor
            def _(pe):
                pe.wait_ge(loaded, 80)
                n = 0
                for w in ("WQ", "WK", "WV"):
                    if n:
                        pe.wait_ge(w_moved, n)
                    for h in range(HEADS):
                        m = nc.tensor.transpose(tx[0:D, h * D:(h + 1) * D], W[w][:, h * D:(h + 1) * D], g.ident[0:D, 0:D])
                    m.then_inc(w_turned, 1)
                    n += 1
                pe.wait_ge(w_moved, 3)
                for n, (l, r) in enumerate((("WQ", "WK"), ("WV", None))):
                    if n:
                        pe.wait_ge(ab_moved, n)
                    for h in range(HEADS):
                        rhs = wT[r][:, h, :] if r else wout[:, h, :]
                        m = nc.tensor.matmul(tx[0:D, h * D:(h + 1) * D], wT[l][:, h, :], rhs, start=True, stop=True)
                    m.then_inc(ab_made, 1)
                pe.wait_ge(ab_moved, 2)
                pe.wait_ge(cleared, 4)

                def prepare(b, k, c):
                    if c == 0:
                        pe.wait_ge(x_staged[k], 16 * (b - k) + 32)
                    pe.wait_ge(tx_moved, 4 * b + c + 1)
                    if c < 2:
                        for q in range(2):
                            m = nc.tensor.matmul(tx[:, q * S:(q + 1) * S], A[:, (2 * c + q) * P:(2 * c + q + 1) * P],
                                                 xs[:, k, :], start=True, stop=True)
                    else:
                        m = nc.tensor.matmul(tx[:], xs[:, k, (c - 2) * P:(c - 1) * P], Bm[:], start=True, stop=True)
                    m.then_inc(tx_full, 1)

                def scores(b, k, n):
                    hp, a = n // TPB, n % TPB
                    if n == 0:
                        pe.wait_ge(tx_moved, 4 * b + 2 + 1)
                    pe.wait_ge(exp_done, 2 * (b * NSTEP + n) + 2)
                    for q, x in enumerate((xs, xlow)):
                        m = nc.tensor.matmul(sc[n % NS][:, q, :], tT[:, k, hp, a * P:(a + 1) * P], x[:, k, :],
                                             start=True, stop=True)
                    m.then_inc(s_full, 1)

                def turn(b, n, slot):
                    pe.wait_ge(probT_ready, b * NSTEP + n + 1)
                    pe.wait_ge(prob_ready, b * NSTEP + n + 1)
                    for q in range(2):
                        for j in range(TPB):
                            m = nc.tensor.transpose(pt[slot][:, q, j, :], prob[:, slot, q, j * P:(j + 1) * P], g.ident[:])
                    m.then_inc(turned, 1)

                def weigh(b, k, hp, slot):
                    pe.wait_ge(probT_ready, b * NSTEP + 2 * hp + 2 + 2)
                    if hp == 0:
                        pe.wait_ge(tx_moved, 4 * b + 4 + 1)
                        pe.wait_ge(oT_ready, b + 1)
                    for q in range(2):
                        for j in range(TPB):
                            m = nc.tensor.matmul(ot, xB[:, k, j, (2 * hp + q) * D:(2 * hp + q + 1) * D],
                                                 probT[:, slot, q, j, :], start=hp + q + j == 0,
                                                 stop=hp == HP - 1 and q == 1 and j == TPB - 1)
                    m.then_inc(pv_done, 1)

                def sequence(b, k, last):
                    for n in range(NSTEP):
                        if n + 2 < NSTEP:
                            scores(b, k, n + 2)
                        elif not last:
                            scores(b + 1, 1 - k, n + 2 - NSTEP)
                        turn(b, n, n % 2)
                        if n % 2 == 1 and n >= 3:
                            weigh(b, k, n // 2 - 1, (n // 2 - 1) % 2)
                        if n < 4 and not last:
                            prepare(b + 1, 1 - k, n)
                    weigh(b, k, HP - 1, (HP - 1) % 2)
                    pe.wait_ge(oT_ready, b + 2)
                    wait_apart(pe, o_added, b + 1, passed)
                    for a in range(TPB):
                        m = nc.tensor.transpose(ott[:, a, :], oT[:, a * P:(a + 1) * P], g.ident[0:D, 0:D])
                    m.then_inc(o_turned, 1)

                for c in range(4):
                    prepare(0, 0, c)
                scores(0, 0, 0)
                scores(0, 0, 1)
                with pe.Fori(0, B // 2 - 1) as i:
                    for k in range(2):
                        sequence(2 * i + k, k, False)
                sequence(B - 2, 0, False)
                sequence(B - 1, 1, True)

            @block.scalar
            def _(act):
                act.sem_inc(exp_done, 2 * NS)
                act.sem_inc(probT_ready, 2)
                act.sem_inc(oT_ready, 1)
                for n, w in enumerate(("WQ", "WK", "WV")):
                    act.wait_ge(w_turned, n + 1)
                    nc.scalar.copy(wT[w].rearrange("d h c -> d (h c)"), tx[0:D, :]).then_inc(w_moved, 1)

                def move_tT(b, k, c):
                    act.wait_ge(tx_full, 4 * b + c + 1)
                    nc.scalar.copy(tT[:, k, 2 * c:2 * c + 2, :].rearrange("p h s -> p (h s)"), tx[:]).then_inc(tx_moved, 1)

                def exps(b, n):
                    act.wait_ge(max_ready, b * NSTEP + n + 1)
                    act.wait_ge(turned, b * NSTEP + n + 1)
                    for q in range(2):
                        nc.scalar.activation(prob[:, n % 2, q, :], sc[n % NS][:, q, :], ACT.Exp,
                                             bias=nm[:, n % 4, q:q + 1], scale=scale,
                                             accum_out=rs[:, n % 4, q:q + 1]).then_inc(exp_done, 1)

                def move_probT(b, n):
                    hp, a = n // TPB, n % TPB
                    act.wait_ge(pv_done, b * HP + hp + 1)
                    act.wait_ge(turned, b * NSTEP + n + 1 + 2)
                    nc.scalar.copy(probT[:, hp % 2, :, :, a * P:(a + 1) * P], pt[n % 2][:]).then_inc(probT_ready, 1)

                def sequence(b, k, last):
                    for n in range(NSTEP):
                        exps(b, n)
                        if n:
                            move_probT(b, n - 1)
                        if n in (1, 2) and not last:
                            move_tT(b + 1, 1 - k, n - 1)
                    move_probT(b, NSTEP - 1)
                    act.wait_ge(o_turned, b + 1)
                    act.wait_ge(pv_done, b * HP + HP + 2)
                    nc.scalar.activation(oT[:], ot, ACT.Identity, bias=bout[:]).then_inc(oT_ready, 1)

                act.wait_ge(ab_moved, 2)
                act.wait_ge(loaded, 80)
                for c in range(2):
                    move_tT(0, 0, c)
                with act.Fori(0, B // 2 - 1) as i:
                    for k in range(2):
                        sequence(2 * i + k, k, False)
                sequence(B - 2, 0, False)
                sequence(B - 1, 1, True)

            @block.vector
            def _(v):
                for t in (xs[D:P], xlow[0:D], A[D:P], Bm[D:P]):
                    nc.vector.memset(t, 0.0).then_inc(cleared, 1)
                v.sem_inc(s_full, 2 * NSTEP)
                v.sem_inc(tx_moved, 1)
                v.sem_inc(turned, 2)
                v.sem_inc(pv_done, 2)
                v.sem_inc(o_turned, 1)
                v.sem_inc(o_added, 1)
                for n, t in enumerate((A, Bm)):
                    v.wait_ge(ab_made, n + 1)
                    nc.vector.tensor_copy(t[0:D, :], tx[0:D, :]).then_inc(ab_moved, 1)

                def move_xB(b, k, j):
                    if not isinstance(b, int) or b:
                        v.wait_ge(pv_done, (b - 1) * HP + 2)
                    v.wait_ge(tx_full, 4 * b + 2 + j + 1)
                    nc.vector.tensor_copy(xB[:, k, j, :], tx[:]).then_inc(tx_moved, 1)

                def maxima(b, n, maxed):
                    v.wait_ge(s_full, b * NSTEP + n + 1 + 2 * NSTEP)
                    nc.vector.tensor_reduce(mx[:, n % 4, :], sc[n % NS][:], AX.X, ALU.max).then_inc(own, 1)
                    v.wait_ge(own, maxed)
                    nc.vector.tensor_scalar(nm[:, n % 4, :], mx[:, n % 4, :], -scale, None, ALU.mult).then_inc(max_ready, 1)

                def normalize(b, n, last_own):
                    v.wait_ge(exp_done, 2 * (b * NSTEP + n + 1) + 2 * NS)
                    nc.vector.reciprocal(rr[:, n % 4, :], rs[:, n % 4, :]).then_inc(own, 1)
                    v.wait_ge(own, last_own)
                    nc.vector.tensor_tensor(prob[:, n % 2], prob[:, n % 2], bc(rr[:, n % 4, :], 2, S), ALU.mult).then_inc(prob_ready, 1)

                def sequence(b, k, last):
                    for n in range(NSTEP):
                        if n + 1 < NSTEP:
                            maxima(b, n + 1, 2 * (b * NSTEP + n) + 2)
                        elif not last:
                            maxima(b + 1, 0, 2 * (b * NSTEP + n) + 2)
                        normalize(b, n, 2 * (b * NSTEP + n) + (2 if last and n == NSTEP - 1 else 3))
                        if n in (3, 4) and not last:
                            move_xB(b + 1, 1 - k, n - 3)
                    v.wait_ge(o_turned, b + 2)
                    h = g.H[:, ds(b * TPB, TPB), :]
                    nc.vector.tensor_tensor(h, h, ott, ALU.add).then_inc(o_added, 1)

                for j in range(2):
                    move_xB(0, 0, j)
                maxima(0, 0, 1)
                with v.Fori(0, B // 2 - 1) as i:
                    for k in range(2):
                        sequence(2 * i + k, k, False)
                sequence(B - 2, 0, False)
                sequence(B - 1, 1, True)


def narrow_attention(nc, g, name, w_qkv, w_proj, b_proj, b_qkv=None, slopes=None, neighbours=31):
    layernorm(nc, g, "ln_" + name, g.H, transposed=True)
    HEADS, DH = 8, D // 8
    linear = slopes is not None
    scale = DH ** -0.5

    def cols(u):
        return slice(u * P, (u + 1) * P) if linear else slice(u, S, 2)

    with Stage(nc, name) as st:
        wqk, wkv, wp = st.sb("wqk", [P, P]), st.sb("wkv", [P, P]), st.sb("wp", [P, D])
        bp = st.sb("bp", [P, D])
        xs = st.sb("xs", [P, 2, S])
        q_s, kT = st.sb("q", [P, 2, S]), st.sb("kT", [P, 2, S])
        Qm = g.X[:].rearrange("p t d -> p (t d)")[:, 0:2 * HEADS * S].rearrange("p (k h s) -> p k h s", k=2, h=HEADS)
        vs = st.sb("vs", [P, 2, 2, D])
        Vm = st.sb("Vm", [P, 2, 2, HEADS, D])
        weights = g.X[:].rearrange("p t d -> p (t d)")[:, 2 * HEADS * S:2 * HEADS * S + 2 * HEADS * P].rearrange(
            "p (u h s) -> p u h s", u=2, h=HEADS)
        oT = st.sb("oT", [P, 2, S])
        out = st.sb("out", [P, TPB, D])
        headsf, headsp = st.sb("headsf", [P, HEADS, D]), st.sb("headsp", [P, HEADS])
        sp_ = [st.ps(f"sp{u}", [P, HEADS, P]) for u in range(2)]
        qkv = st.ps("qkv", [P, 512])
        ob = st.ps("ob", [P, 512])
        qkp, vp = qkv[:, 0:S], qkv[:, S:512].rearrange("p (u c) -> p u c", u=2)
        otp, pp = ob[0:D, 0:S], ob[:, S:S + TPB * D].rearrange("p (a d) -> p a d", d=D)
        if linear:
            vp = st.ps("vp", [P, 2, S // 2])
            stp = st.ps("stp", [D, D])[:]
            decay = st.sb("decay", [P, HEADS, P])
            dist = st.sb("dist", [P, P])
            nslope, nslope_p = st.sb("nslope", [P, HEADS]), st.sb("nslope_p", [P, 1])
            kdec, qdec_t = st.sb("kdec", [P, HEADS]), st.sb("qdec_t", [P, P])
            tmp8, mine, left = st.sb("tmp8", [P, HEADS]), st.sb("mine", [P, HEADS]), st.sb("left", [P, 1])
            pos = st.sb("pos", [P, P])
            Kd, state, qd = st.sb("Kd", [P, D]), st.sb("state", [P, D]), st.sb("qd", [P, 2, P])
        else:
            mask = st.sb("mask", [P, 4, P], BF16)
            maskf = st.sb("maskf", [P, P])
            prob = st.sb("prob", [P, 2, HEADS, P])
            bq, bk, bv = st.sb("bq", [D, 1]), st.sb("bk", [D, 1]), st.sb("bv", [P, D])
            mx, nm, rs, rr = (st.sb(n, [P, 2, HEADS]) for n in ("mx", "nm", "rs", "rr"))
            pt = st.ps("pt", [P, HEADS, P])
        names = ("loaded", "cleared", "built", "passed", "qkv_full", "qk_moved", "v_ready", "vm_ready",
                 "qm_ready", "s_full", "s_read", "w_ready", "pv_done", "o_moved", "proj_done", "added", "vec_own")
        (loaded, cleared, built, passed, qkv_full, qk_moved, v_ready, vm_ready, qm_ready, s_full, s_read,
         w_ready, pv_done, o_moved, proj_done, added, own) = (st.sem(n) for n in names)
        x_staged = [st.sem(f"x_staged{k}") for k in range(2)]
        if linear:
            tabs, exped, state_full, state_ready, qd_ready, kd_ready = (
                st.sem(n) for n in ("tabs", "exped", "state_full", "state_ready", "qd_ready", "kd_ready"))
        else:
            max_ready, normed, turned, maxed, inverted = (
                st.sem(n) for n in ("max_ready", "normed", "turned", "maxed", "inverted"))
        LOADS = 4 + (1 if linear else 3)
        zeroed = [(t, 0.0) for t in (wqk[D:P], wkv[D:P], wp[D:P], xs[D:P], kT[D:P], oT[D:P], Qm[D:P, 0], Qm[D:P, 1])]
        zeroed += [(state[D:P], 0.0), (qd[D:P], 0.0)] if linear else [(maskf[:], 0.0)]
        ones = [(headsf[:], 1.0), (headsp[:], 1.0)]
        NCLEAR = len(zeroed + ones)
        NBUILT = 4 + (2 if linear else 3)

        def pipeline(eng, sequence):
            sequence(0, 0, first=True)
            sequence(1, 1)
            with eng.Fori(0, B // 2 - 2) as i:
                for k in range(2):
                    sequence(2 * i + 2 + k, k)
            sequence(B - 2, 0)
            sequence(B - 1, 1, last=True)

        with nc.Block() as block:
            @block.sync
            def _(sp):
                sp.dma_start(wqk[0:D, :], w_qkv[:, 0:2 * D]).then_inc(loaded, 16)
                sp.dma_start(wkv[0:D, :], w_qkv[:, D:3 * D]).then_inc(loaded, 16)
                sp.dma_start(wp[0:D, :], w_proj).then_inc(loaded, 16)
                sp.dma_start(bp[:], b_proj.partition_broadcast(P)).then_inc(loaded, 16)
                if linear:
                    sp.dma_start(nslope[:], slopes.partition_broadcast(P)).then_inc(loaded, 16)
                else:
                    sp.dma_start(bq[:], b_qkv[0:D].unsqueeze(1)).then_inc(loaded, 16)
                    sp.dma_start(bk[:], b_qkv[D:2 * D].unsqueeze(1)).then_inc(loaded, 16)
                    sp.dma_start(bv[:], b_qkv[2 * D:3 * D].partition_broadcast(P)).then_inc(loaded, 16)
                sp.wait_ge(cleared, NCLEAR)
                with sp.Fori(0, B // 2) as i:
                    for k in range(2):
                        sp.wait_ge(qkv_full, 2 * i + k + 1)
                        sp.dma_start(xs[0:D, k, :], g.XT[0:D, ds((2 * i + k) * S, S)]).then_inc(x_staged[k], 16)

            @block.gpsimd
            def _(pool):
                n = [0]

                def then(ins):
                    n[0] += 1
                    ins.then_inc(built, 1)
                    pool.wait_ge(built, n[0])

                pool.wait_ge(cleared, NCLEAR)
                for t, pat, mul in ((headsf[:], [[-DH, HEADS], [1, D]], 0), (headsp[:], [[-DH, HEADS]], 1)):
                    then(nc.gpsimd.affine_select(out=t, in_=t, compare_op=ALU.is_ge, fill=0.0, base=0, pattern=pat,
                                                 channel_multiplier=mul))
                    then(nc.gpsimd.affine_select(out=t, in_=t, compare_op=ALU.is_ge, fill=0.0, base=DH - 1,
                                                 pattern=[[-a, c] for a, c in pat], channel_multiplier=-mul))
                if linear:
                    then(nc.gpsimd.iota(dist[:], pattern=[[1, P]], base=0, channel_multiplier=-1,
                                        allow_small_or_imprecise_dtypes=True))
                    then(nc.gpsimd.iota(pos[:], pattern=[[1, P]], base=0, channel_multiplier=0,
                                        allow_small_or_imprecise_dtypes=True))
                    pool.wait_ge(exped, HEADS)
                    nc.gpsimd.affine_select(out=decay[:], in_=decay[:], compare_op=ALU.is_ge, fill=0.0, base=0,
                                            pattern=[[0, HEADS], [1, P]], channel_multiplier=-1).then_inc(tabs, 1)
                else:
                    r, short = neighbours // 2, P - neighbours
                    lo, hi = maskf[:, 0:short], maskf[:, neighbours:P]
                    then(nc.gpsimd.affine_select(out=lo, in_=lo, compare_op=ALU.is_ge, fill=-BIG, base=r,
                                                 pattern=[[1, short]], channel_multiplier=-1))
                    then(nc.gpsimd.affine_select(out=hi, in_=hi, compare_op=ALU.is_ge, fill=-BIG, base=r - neighbours,
                                                 pattern=[[-1, short]], channel_multiplier=1))
                    then(nc.gpsimd.tensor_copy(mask[:], bc(maskf[:], 1, 4)))
                assert n[0] == NBUILT

                def mask_values(b, k):
                    pool.wait_ge(pv_done, 2 * b + 2)
                    for u in range(2):
                        pool.wait_ge(v_ready, 2 * b + u + 1 + 2)
                        nc.gpsimd.tensor_tensor(Vm[:, k, u], bc(vs[:, k, u, :], 1, HEADS), headsf[:], ALU.mult).then_inc(vm_ready, 1)

                with pool.Fori(0, B // 2) as i:
                    for k in range(2):
                        mask_values(2 * i + k, k)

            @block.tensor
            def _(pe):
                pe.wait_ge(loaded, 16 * LOADS)
                pe.wait_ge(cleared, NCLEAR)
                pe.wait_ge(built, NBUILT)
                pe.sem_inc(qkv_full, 2)
                pe.sem_inc(pv_done, 4)

                def setup(b, k):
                    pe.wait_ge(x_staged[k], 8 * (b - k) + 16)
                    pe.wait_ge(qk_moved, 2 * b + 2)
                    pe.wait_ge(v_ready, 2 * b + 2)
                    if linear:
                        pe.wait_ge(kd_ready, b + 1)
                    nc.tensor.matmul(qkp, wqk[:], xs[:, k, :], start=True, stop=True)
                    for u in range(2):
                        m = nc.tensor.matmul(vp[:, u, :], xs[:, k, cols(u)], wkv[:], start=True, stop=True)
                    m.then_inc(qkv_full, 1)

                def scores(b, k, u):
                    pe.wait_ge(w_ready if linear else s_read, 2 * b + u + 1)
                    pe.wait_ge(qk_moved, 2 * b + 4)
                    pe.wait_ge(qm_ready, b + 1)
                    if linear:
                        for f in range(2):
                            m = nc.tensor.matmul(sp_[u][:, 4 * f:4 * f + 4, :], kT[:, k, cols(u)],
                                                 Qm[:, k, 4 * f:4 * f + 4, cols(u)], start=True, stop=True)
                    else:
                        for f in range(2):
                            nc.tensor.matmul(sp_[u][:, 4 * f:4 * f + 4, :], g.identb[:], mask[:], start=True, stop=False)
                            for h in range(4 * f, 4 * f + 4):
                                m = nc.tensor.matmul(sp_[u][:, h, :], Qm[:, k, h, cols(u)], kT[:, k, cols(u)],
                                                     start=False, stop=h % 4 == 3)
                    m.then_inc(s_full, 1)

                def turn(b, u):
                    pe.wait_ge(normed, 2 * b + u + 1)
                    pe.wait_ge(w_ready, 2 * b + u + 1)
                    for h in range(HEADS):
                        m = nc.tensor.transpose(pt[:, h, :], prob[:, u, h, :], g.ident[:])
                    m.then_inc(turned, 1)

                def carry(b, k):
                    pe.wait_ge(state_ready, b + 1)
                    pe.wait_ge(kd_ready, b + 2)
                    pe.wait_ge(v_ready, 2 * b + 1 + 2)
                    nc.tensor.matmul(stp, Kd[:], vs[:, k, 0, :], start=True, stop=True).then_inc(state_full, 1)

                def weigh(b, k, u):
                    pe.wait_ge(o_moved, 2 * b + u + 2)
                    if u == 0:
                        pe.wait_ge(added, b + 1)
                    pe.wait_ge(vm_ready, 2 * b + u + 1 + 4)
                    first = True
                    if linear and u == 1:
                        pe.wait_ge(qd_ready, b + 1)
                        pe.wait_ge(state_ready, b + 2)
                        nc.tensor.matmul(otp[:, u * P:(u + 1) * P], state[:], qd[:, k, :], start=True, stop=False)
                        first = False
                    pe.wait_ge(w_ready, 2 * b + u + 1 + (2 if linear else 1))
                    for h in range(HEADS):
                        m = nc.tensor.matmul(otp[:, u * P:(u + 1) * P], Vm[:, k, u, h, :], weights[:, u, h, :],
                                             start=first, stop=h == HEADS - 1)
                        first = False
                    m.then_inc(pv_done, 1)

                def project(b, k):
                    pe.wait_ge(o_moved, 2 * b + 2 + 2)
                    for a in range(TPB):
                        m = nc.tensor.matmul(pp[:, a, :], oT[:, k, a * P:(a + 1) * P], wp[:], start=True, stop=True)
                    m.then_inc(proj_done, 1)

                def sequence(b, k, first=False, last=False):
                    if linear:
                        carry(b, k)
                        scores(b, k, 1)
                        if not last:
                            setup(b + 1, 1 - k)
                        weigh(b, k, 0)
                        weigh(b, k, 1)
                        if not last:
                            scores(b + 1, 1 - k, 0)
                        project(b, k)
                    else:
                        if not last:
                            setup(b + 1, 1 - k)
                        scores(b, k, 1)
                        turn(b, 0)
                        if not first:
                            weigh(b - 1, 1 - k, 1)
                        if not last:
                            scores(b + 1, 1 - k, 0)
                        if not first:
                            project(b - 1, 1 - k)
                        turn(b, 1)
                        weigh(b, k, 0)
                        if last:
                            weigh(b, k, 1)
                            project(b, k)

                setup(0, 0)
                scores(0, 0, 0)
                pipeline(pe, sequence)

            @block.scalar
            def _(act):
                act.wait_ge(loaded, 16 * LOADS)
                act.wait_ge(cleared, NCLEAR)
                act.sem_inc(qk_moved, 2)
                act.sem_inc(o_moved, 2)
                if linear:
                    act.wait_ge(tabs, 4)
                    for h in range(HEADS):
                        nc.scalar.activation(decay[:, h, :], dist[:], ACT.Exp, scale=nslope[:, h:h + 1]).then_inc(exped, 1)
                    nc.scalar.activation(kdec[:], tmp8[:], ACT.Exp).then_inc(exped, 1)
                    nc.scalar.activation(qdec_t[0:D], pos[0:D], ACT.Exp, scale=nslope_p[0:D]).then_inc(exped, 1)
                else:
                    act.sem_inc(s_read, 2)
                    act.sem_inc(w_ready, 1)

                def move_qk(b, k):
                    act.wait_ge(qkv_full, b + 1 + 2)
                    act.wait_ge(s_full, 2 * b + 2)
                    if linear:
                        nc.scalar.mul(q_s[0:D, k, :], qkp[0:D], scale).then_inc(qk_moved, 1)
                        nc.scalar.copy(kT[0:D, k, :], qkp[D:P]).then_inc(qk_moved, 1)
                    else:
                        nc.scalar.activation(q_s[0:D, k, :], qkp[0:D], ACT.Identity, bias=bq[:]).then_inc(qk_moved, 1)
                        nc.scalar.activation(kT[0:D, k, :], qkp[D:P], ACT.Identity, bias=bk[:]).then_inc(qk_moved, 1)

                def exps(b, u):
                    act.wait_ge(max_ready, 2 * b + u + 1)
                    act.wait_ge(turned, 2 * b + u + 1)
                    for h in range(HEADS):
                        m = nc.scalar.activation(prob[:, u, h, :], sp_[u][:, h, :], ACT.Exp, bias=nm[:, u, h:h + 1],
                                                 scale=scale, accum_out=rs[:, u, h:h + 1])
                    m.then_inc(s_read, 1)

                def move_weights(b, u):
                    act.wait_ge(pv_done, 2 * b + u + 3)
                    act.wait_ge(turned, 2 * b + u + 1 + 2)
                    nc.scalar.copy(weights[:, u], pt[:]).then_inc(w_ready, 1)

                def move_o(b, k, u):
                    act.wait_ge(proj_done, b + 1)
                    act.wait_ge(pv_done, 2 * b + u + 1 + 4)
                    nc.scalar.copy(oT[0:D, k, cols(u)], otp[:, u * P:(u + 1) * P]).then_inc(o_moved, 1)

                def sequence(b, k, first=False, last=False):
                    if not last:
                        move_qk(b + 1, 1 - k)
                    if linear:
                        move_o(b, k, 0)
                        move_o(b, k, 1)
                    else:
                        move_weights(b, 0)
                        exps(b, 1)
                        if not first:
                            move_o(b - 1, 1 - k, 1)
                        move_weights(b, 1)
                        if not last:
                            exps(b + 1, 0)
                        move_o(b, k, 0)
                        if last:
                            move_o(b, k, 1)

                move_qk(0, 0)
                if not linear:
                    exps(0, 0)
                pipeline(act, sequence)

            @block.vector
            def _(v):
                for t, value in zeroed + ones:
                    nc.vector.memset(t, value).then_inc(cleared, 1)
                v.wait_ge(cleared, NCLEAR)
                v.wait_ge(loaded, 16 * LOADS)
                v.wait_ge(built, NBUILT)
                v.sem_inc(s_full, 4)
                v.sem_inc(v_ready, 2)
                v.sem_inc(vm_ready, 4)
                v.sem_inc(proj_done, 2)
                v.sem_inc(added, 1)
                if linear:
                    v.sem_inc(w_ready, 2)
                    v.sem_inc(kd_ready, 1)
                    v.sem_inc(state_ready, 1)
                    link = chain(v, own)
                    nc.vector.tensor_scalar(nslope[:], nslope[:], -1.0, None, ALU.mult).then_inc(tabs, 1)
                    nc.vector.tensor_scalar(dist[:], dist[:], 0.0, None, ALU.max).then_inc(tabs, 1)
                    v.wait_ge(tabs, 2)
                    link(nc.vector.tensor_scalar(left[:], g.lane[:], -1.0, float(P), ALU.mult, ALU.add))
                    nc.vector.tensor_scalar(tmp8[:], nslope[:], left[:], None, ALU.mult).then_inc(tabs, 1)
                    link(nc.vector.tensor_tensor(mine[:], nslope[:], headsp[:], ALU.mult))
                    nc.vector.reduce_sum(nslope_p[:], mine[:], AX.X).then_inc(tabs, 1)
                    v.wait_ge(exped, HEADS + 2)
                    v.wait_ge(tabs, 5)
                else:
                    v.sem_inc(turned, 2)

                def maxima(b, u):
                    v.wait_ge(s_full, 2 * b + u + 1 + 4)
                    nc.vector.tensor_reduce(mx[:, u], sp_[u][:], AX.X, ALU.max).then_inc(maxed, 1)
                    v.wait_ge(maxed, 2 * b + u + 1)
                    nc.vector.tensor_scalar(nm[:, u], mx[:, u], -scale, None, ALU.mult).then_inc(max_ready, 1)

                def normalize(b, u):
                    v.wait_ge(s_read, 2 * b + u + 1 + 2)
                    nc.vector.reciprocal(rr[:, u], rs[:, u]).then_inc(inverted, 1)
                    v.wait_ge(inverted, 2 * b + u + 1)
                    nc.vector.tensor_tensor(prob[:, u], prob[:, u], bc(rr[:, u], 2, P), ALU.mult).then_inc(normed, 1)

                def take_v(b, k):
                    v.wait_ge(qkv_full, b + 1 + 2)
                    if not linear:
                        v.wait_ge(qk_moved, 2 * b + 4)
                    v.wait_ge(vm_ready, 2 * b + 2)
                    for u in range(2):
                        if linear:
                            nc.vector.tensor_copy(vs[:, k, u, :], vp[:, u, D:2 * D]).then_inc(v_ready, 1)
                        else:
                            nc.vector.tensor_tensor(vs[:, k, u, :], vp[:, u, D:2 * D], bv[:], ALU.add).then_inc(v_ready, 1)
                    if linear:
                        if not (isinstance(b, int) and b == 0):
                            v.wait_ge(state_full, b)
                        nc.vector.tensor_tensor(Kd[:].rearrange("p (h d) -> p h d", h=HEADS),
                                                vp[:, 0, 0:D].rearrange("p (h d) -> p h d", h=HEADS),
                                                bc(kdec[:], 2, DH), ALU.mult).then_inc(kd_ready, 1)

                def mask_queries(b, k):
                    v.wait_ge(qk_moved, 2 * b + 2 + 2)
                    v.wait_ge(s_full, 2 * b + 2)
                    nc.vector.tensor_tensor(Qm[0:D, k], bc(q_s[0:D, k, :], 1, HEADS), bc(headsp[0:D], 2, S),
                                            ALU.mult).then_inc(qm_ready, 1)
                    if linear:
                        v.wait_ge(pv_done, 2 * b + 2)
                        nc.vector.tensor_tensor(qd[0:D, k, :], q_s[0:D, k, P:S], qdec_t[0:D], ALU.mult).then_inc(qd_ready, 1)

                def decayed(b, u):
                    v.wait_ge(s_full, 2 * b + u + 1 + 4)
                    v.wait_ge(pv_done, 2 * b + u + 3)
                    nc.vector.tensor_tensor(weights[:, u], sp_[u][:], decay[:], ALU.mult).then_inc(w_ready, 1)

                def take_state(b):
                    v.wait_ge(state_full, b + 1)
                    v.wait_ge(pv_done, 2 * b + 4)
                    nc.vector.tensor_tensor(state[0:D].rearrange("p (h d) -> p h d", h=HEADS),
                                            stp.rearrange("p (h d) -> p h d", h=HEADS), bc(headsp[0:D], 2, DH),
                                            ALU.mult).then_inc(state_ready, 1)

                def add(b):
                    v.wait_ge(proj_done, b + 1 + 2)
                    nc.vector.tensor_tensor(out[:], pp, bc(bp[:], 1, TPB), ALU.add).then_inc(added, 1)
                    v.wait_ge(added, b + 2)
                    h = g.H[:, ds(b * TPB, TPB), :]
                    nc.vector.tensor_tensor(h, h, out[:], ALU.add).then_inc(own, 1)

                def sequence(b, k, first=False, last=False):
                    if linear:
                        decayed(b, 0)
                        take_state(b)
                        decayed(b, 1)
                    else:
                        normalize(b, 0)
                        maxima(b, 1)
                    if not last:
                        take_v(b + 1, 1 - k)
                        mask_queries(b + 1, 1 - k)
                    if linear:
                        add(b)
                    else:
                        normalize(b, 1)
                        if not last:
                            maxima(b + 1, 0)
                        if not first:
                            add(b - 1)
                        if last:
                            v.wait_ge(own, B - 1)
                            add(b)

                take_v(0, 0)
                mask_queries(0, 0)
                if not linear:
                    maxima(0, 0)
                pipeline(v, sequence)


def attn1(nc, g, I):
    narrow_attention(nc, g, "attn1", I["L1_attn_w_qkv"], I["L1_attn_w_proj"], I["L1_attn_b_proj"],
                     b_qkv=I["L1_attn_b_qkv"])


def attn3(nc, g, I):
    narrow_attention(nc, g, "attn3", I["L3_attn_w_qkv"], I["L3_attn_w_proj"], I["L3_attn_b_proj"],
                     slopes=I["L3_attn_slopes"])


def route_sequences(nc, g, name, Wr, br, E):
    capacity = float(-(-TOKENS * 5 // (4 * E)))
    with Stage(nc, name) as st:
        w, bias = st.sb("w", [P, E]), st.sb("bias", [B, E])
        mean = st.sb("mean", [P, B])
        rw, load, hot, tmp, gt = (st.sb(n, [B, 1, E]) for n in ("rw", "load", "hot", "tmp", "gt"))
        mx, rs = st.sb("mx", [B, 1]), st.sb("rs", [B, 1])
        diag = st.sb("diag", [B, B, E])
        G = st.sb("G", [P, TILES, E])
        rest = st.sb("rest", [P, TILES, E])
        small = st.ps("small", [P, 2, E])
        spread = st.ps("spread", [P, B, E])
        loaded, cleared, own = st.sem("loaded"), st.sem("cleared"), st.sem("vec_own")
        mean_ready, product, probs_ready, diag_ready = (st.sem(n) for n in ("mean_ready", "product", "probs_ready", "diag_ready"))
        shifted, exped = st.sem("shifted"), st.sem("exped")
        gates = GateSplit(nc, g, st, E, rest[:])
        with nc.Block() as block:
            parts = {}

            @block.sync
            def _(sp):
                sp.dma_start(w[0:D, :], Wr).then_inc(loaded, 16)
                sp.dma_start(bias[:], br.partition_broadcast(B)).then_inc(loaded, 16)

            @block.tensor
            def _(pe):
                pe.wait_ge(loaded, 32)
                pe.wait_ge(mean_ready, 1)
                nc.tensor.matmul(small[0:B, 0, :], mean[:], w[:], start=True, stop=True).then_inc(product, 1)
                pe.wait_ge(probs_ready, 1)
                nc.tensor.matmul(small[0:B, 1, :], g.ones[0:B, 0:B], rw[:, 0, :], start=True, stop=True).then_inc(product, 1)
                pe.wait_ge(diag_ready, 1)
                nc.tensor.matmul(spread[:], g.ones[0:B, :], diag[:], start=True, stop=True).then_inc(product, 1)
                gates.tensor(pe)

            @block.vector
            def _(v):
                link = chain(v, own)

                def softmax(turn):
                    link(nc.vector.tensor_reduce(mx[:], rw[:], AX.XY, ALU.max))
                    nc.vector.tensor_scalar(rw[:], rw[:], mx[:], None, ALU.subtract).then_inc(shifted, 1)
                    v.wait_ge(exped, turn)
                    link(nc.vector.tensor_reduce(rs[:], rw[:], AX.XY, ALU.add))
                    link(nc.vector.reciprocal(rs[:], rs[:]))

                nc.vector.memset(w[D:P, :], 0.0).then_inc(cleared, 1)
                link(nc.vector.memset(mean[D:P, :], 0.0))
                link(nc.vector.reduce_sum(mean[0:D, :], g.XT[0:D, :].rearrange("d (b s) -> d b s", s=S), AX.X))
                v.wait_ge(cleared, 1)
                nc.vector.tensor_scalar(mean[0:D, :], mean[0:D, :], 1.0 / S, None, ALU.mult).then_inc(mean_ready, 1)
                v.wait_ge(loaded, 32)
                v.wait_ge(product, 1)
                link(nc.vector.tensor_tensor(rw[:, 0, :], small[0:B, 0, :], bias[:], ALU.add))
                softmax(1)
                nc.vector.tensor_scalar(rw[:], rw[:], rs[:], None, ALU.mult).then_inc(probs_ready, 1)
                v.wait_ge(product, 2)
                link(nc.vector.tensor_scalar(load[:, 0, :], small[0:B, 1, :], float(S), None, ALU.mult))
                link(nc.vector.reciprocal(load[:], load[:]))
                link(nc.vector.tensor_scalar(load[:], load[:], capacity, 1.0, ALU.mult, ALU.min))
                link(nc.vector.tensor_tensor(rw[:], rw[:], load[:], ALU.mult))
                softmax(2)
                link(nc.vector.tensor_scalar(rw[:], rw[:], rs[:], None, ALU.mult))
                vec, parts["pool"], parts["act"] = top2_steps(nc, v, link, st, rw[:], gt[:], E, hot[:], tmp[:])
                vec()
                nc.vector.tensor_tensor(diag[:], bc(g.ident[0:B, 0:B], 2, E), bc(gt[:, 0, :], 1, B), ALU.mult).then_inc(diag_ready, 1)
                v.wait_ge(product, 3)
                link(nc.vector.tensor_copy(G[:].rearrange("p (b a) e -> p b a e", a=TPB), bc(spread[:], 2, TPB)))
                gates.vector(link, G[:])

            @block.gpsimd
            def _(pool):
                parts["pool"](pool)
                gates.gpsimd()

            @block.scalar
            def _(act):
                for turn in range(2):
                    act.wait_ge(shifted, turn + 1)
                    nc.scalar.activation(rw[:], rw[:], ACT.Exp).then_inc(exped, 1)
                parts["act"](act)
                gates.scalar(act)


def ffn1(nc, g, I):
    layernorm(nc, g, "ln_f1", g.H, keep=g.X, transposed=True)
    route_sequences(nc, g, "route1", I["L1_ffn_Wr"], I["L1_ffn_br"], 8)
    experts(nc, g, "experts1", I["L1_ffn_W1"], I["L1_ffn_W2"], I["L1_ffn_b1"], I["L1_ffn_b2"], target=g.X)
    layernorm(nc, g, "ln_out1", g.X, I["L1_ffn_gamma"], I["L1_ffn_beta"], add=g.H)


EDGES = 262144
ROW = EDGES // P
KEY_BASE = 0x20000000
NODE_BITS = 14
LOW = TOKENS - 1


def sort_edges(nc, g, keys, edges):
    NB = ROW // P
    ROW_BITS = ROW.bit_length() - 1
    LEVELS = EDGES.bit_length() - 1
    flat = g.X[:].rearrange("p t d -> p (t d)")
    with Stage(nc, "sort") as st:
        dst = st.sb("dst", [P, ROW], I32)
        lane_i, bits = st.sb("lane_i", [P, 1], I32), st.sb("bits", [P, 1], I32)
        sign = st.sb("sign", [P, LEVELS + 1])
        flip = st.sb("flip", [P, LEVELS + 1])
        bufs = [keys, flat[:, ROW:2 * ROW]]
        signed = flat[:, 2 * ROW:3 * ROW]
        steps = ROW_BITS * (ROW_BITS + 1) // 2
        place, start = [], [steps % 2]
        for k in range(ROW_BITS + 1, LEVELS + 1):
            first = (start[-1] + k - ROW_BITS) % 2
            place.append((first, (first + ROW_BITS) % 2))
            start.append(place[-1][1])
        current = [bufs[s] for s in start]
        across = [bufs[first] for first, _ in place]
        T, back = st.ps("T", [P, NB, P]), st.ps("back", [P, NB, P])
        landed = flat[:, 3 * ROW:4 * ROW]
        loaded, own, ready, turned, flipped, copied = (
            st.sem(n) for n in ("loaded", "vec_own", "ready", "turned", "flipped", "copied"))

        def halves(buf, half):
            s = buf.rearrange("p (n two h) -> p n two h", two=2, h=half)
            return s[:, :, 0, :], s[:, :, 1, :]
        with nc.Block() as block:
            @block.sync
            def _(sp):
                rows = edges.rearrange("two (p f) -> two p f", p=P)
                sp.dma_start(bufs[0].bitcast(I32), rows[0]).then_inc(loaded, 16)
                sp.dma_start(dst[:], rows[1]).then_inc(loaded, 16)

            @block.scalar
            def _(act):
                for n, k in enumerate(range(ROW_BITS + 1, LEVELS + 1)):
                    act.wait_ge(ready, 2 * n + 1)
                    if n:
                        act.wait_ge(turned, 2 * n)
                    nc.scalar.activation(signed, current[n], ACT.Copy, scale=flip[:, k:k + 1]).then_inc(flipped, 1)
                    for part, (bank, half) in enumerate(((T, 1 << (k - ROW_BITS - 1)), (back, ROW // 2))):
                        act.wait_ge(turned, 2 * n + part + 1)
                        act.wait_ge(ready, 2 * n + part + 1)
                        nc.scalar.copy(halves(landed, half)[1], halves(bank[:].rearrange("p c q -> p (c q)"), half)[1]).then_inc(copied, 1)

            @block.tensor
            def _(pe):
                for n in range(LEVELS - ROW_BITS):
                    pe.wait_ge(flipped, n + 1)
                    for c in range(NB):
                        m = nc.tensor.transpose(T[:, c, :], signed[:, c * P:(c + 1) * P], g.ident[:])
                    m.then_inc(turned, 1)
                    pe.wait_ge(ready, 2 * n + 2)
                    for c in range(NB):
                        m = nc.tensor.transpose(back[:, c, :], across[n][:, c * P:(c + 1) * P], g.ident[:])
                    m.then_inc(turned, 1)

            @block.vector
            def _(v):
                link = chain(v, own)
                at = [0]

                def put():
                    at[0] ^= 1
                    return bufs[at[0]]

                def step(src, half, mirrored=False, done=None, second=None):
                    low, high = halves(put(), half)
                    a, b = halves(src, half)
                    if mirrored:
                        b = b[:, :, ::-1]
                    if second is not None:
                        b = halves(second, half)[1]
                    nc.vector.tensor_tensor(low, a, b, ALU.min)
                    last = nc.vector.tensor_tensor(high, a, b, ALU.max)
                    if done is None:
                        link(last)
                    else:
                        last.then_inc(done, 1)
                    return bufs[at[0]]

                link(nc.vector.tensor_copy(lane_i[:], g.lane[:]))
                link(nc.vector.memset(sign[:], 1.0))
                for k in range(ROW_BITS, LEVELS):
                    link(nc.vector.tensor_scalar(bits[:], lane_i[:], k - ROW_BITS, 1, ALU.logical_shift_right, ALU.bitwise_and))
                    link(nc.vector.tensor_copy(sign[:, k:k + 1], bits[:]))
                    link(nc.vector.tensor_scalar(sign[:, k:k + 1], sign[:, k:k + 1], -2.0, 1.0, ALU.mult, ALU.add))
                link(nc.vector.tensor_tensor(flip[:, 1:], sign[:, 1:], sign[:, :-1], ALU.mult))
                v.wait_ge(loaded, 32)
                k0 = bufs[0].bitcast(I32)
                link(nc.vector.tensor_scalar(dst[:], dst[:], NODE_BITS, KEY_BASE, ALU.logical_shift_left, ALU.bitwise_or))
                link(nc.vector.tensor_tensor(k0, k0, dst[:], ALU.bitwise_or))
                link(nc.vector.tensor_scalar(bufs[0], bufs[0], sign[:, ROW_BITS:ROW_BITS + 1], None, ALU.mult))
                data = bufs[0]
                for k in range(1, ROW_BITS + 1):
                    for j in range(k - 1, -1, -1):
                        data = step(data, 1 << j, mirrored=j == k - 1,
                                    done=ready if k == ROW_BITS and j == 0 else None)
                for n, k in enumerate(range(ROW_BITS + 1, LEVELS + 1)):
                    v.wait_ge(copied, 2 * n + 1)
                    data = T[:].rearrange("p c q -> p (c q)")
                    for j in range(k - ROW_BITS - 1, -1, -1):
                        data = step(data, 1 << j, done=ready if j == 0 else None,
                                    second=landed if j == k - ROW_BITS - 1 else None)
                    assert data is bufs[place[n][0]]
                    v.wait_ge(copied, 2 * n + 2)
                    data = back[:].rearrange("p c q -> p (c q)")
                    for j in range(ROW_BITS - 1, -1, -1):
                        data = step(data, 1 << j, done=ready if j == 0 and k < LEVELS else None,
                                    second=landed if j == ROW_BITS - 1 else None)
                    assert data is bufs[place[n][1]]
                if data is not keys:
                    nc.vector.tensor_copy(keys, data).then_inc(own, 1)


HEADS2, CH = 4, 16
TAB = CH + HEADS2
ST = 2 * HEADS2 + CH


class Gat:

    def __init__(self, nc, g, ctx):
        def sb(name, shape, dt=F32):
            return ctx.enter_context(nc.sbuf_tensor("gat_" + name, shape, dt))

        flat = g.X[:].rearrange("p t d -> p (t d)")
        self.keys, self.dst, self.src_row, self.keep = (flat[:, n * ROW:(n + 1) * ROW] for n in range(4))
        self.start_row, self.end_row, self.carry_row = (sb(n, [P, TILES], I32) for n in ("start_row", "end_row", "carry_row"))
        self.first_row = sb("first_row", [P, 1], I32)
        self.table = sb("table", [P, TILES, TAB])
        self.a_dst = sb("a_dst", [P, TILES, HEADS2])
        self.t_table = nc.dram_tensor("gat_node_table", [TOKENS, TAB], F32).ap()
        self.t_dst = nc.dram_tensor("gat_dst_table", [TOKENS, HEADS2], F32).ap()
        self.t_starts = nc.dram_tensor("gat_starts", [EDGES + TOKENS, HEADS2], F32).ap()
        self.t_state = nc.dram_tensor("gat_states", [EDGES + 1, ST], F32).ap()
        self.t_carry = nc.dram_tensor("gat_carries", [P, ST], F32).ap()
        self.t_edge_dst = nc.dram_tensor("gat_row_ends", [2, P], I32).ap()


def table_row(v, link, out, node, tmp):
    link(v.tensor_scalar(out, node, P - 1, 7, ALU.bitwise_and, ALU.logical_shift_left))
    link(v.tensor_scalar(tmp, node, 7, P - 1, ALU.logical_shift_right, ALU.bitwise_and))
    link(v.tensor_tensor(out, out, tmp, ALU.bitwise_or))


def locate_runs(nc, g, q):
    COLS = 16
    SPREAD = (COLS, COLS // 2)
    with Stage(nc, "runs") as st:
        low, high = q.src_row, q.keep
        lane = st.sb("iota", [P, COLS, P], BF16)
        ones, tri = st.sb("zeros", [P, P], BF16), st.sb("tri", [P, P])
        spread, hot = (g.GT[:, n * 4 * COLS * P:(n + 1) * 4 * COLS * P].rearrange(
            "p (k s c v) -> p k s c v", k=2, s=2, v=P) for n in range(2))
        cnt, tot, cum, start, has, end, node, a, b = (
            st.sb(n, [P, TILES]) for n in ("cnt", "tot", "cum", "start", "has", "end", "node", "a", "b"))
        ai, bi = st.sb("ai", [P, TILES], I32), st.sb("bi", [P, TILES], I32)
        ends = st.sb("ends", [P, 2], I32)
        first_tmp = st.sb("first_tmp", [P, 1], I32)
        count_p, sums_p = st.ps("count", [P, P]), st.ps("sums", [P, 2, TILES])
        own, made, values_ready, spread_ready, hot_ready, counted, passed, copied, summed, ends_ready, ends_out = (
            st.sem(n) for n in ("vec_own", "made", "values_ready", "spread_ready", "hot_ready", "counted", "pe_passed",
                                "copied", "summed", "ends_ready", "ends_out"))
        NI = ROW // (2 * COLS)
        with nc.Block() as block:
            @block.gpsimd
            def _(pool):
                nc.gpsimd.iota(lane[:], pattern=[[0, COLS], [1, P]], base=0, channel_multiplier=0,
                               allow_small_or_imprecise_dtypes=True).then_inc(made, 1)
                nc.gpsimd.memset(ones[:].bitcast(F32), 0.0).then_inc(made, 1)
                nc.gpsimd.memset(tri[:], 1.0).then_inc(made, 1)
                nc.gpsimd.iota(node[:], pattern=[[P, TILES]], base=0, channel_multiplier=1,
                               allow_small_or_imprecise_dtypes=True).then_inc(made, 1)
                pool.wait_ge(made, 4)
                nc.gpsimd.affine_select(out=tri[:], in_=tri[:], compare_op=ALU.is_gt, fill=0.0, base=0,
                                        pattern=[[1, P]], channel_multiplier=-1).then_inc(made, 1)

            @block.tensor
            def _(pe):
                pe.wait_ge(made, 5)
                pe.sem_inc(counted, 2)
                nc.tensor.matmul(count_p[:], ones[:], ones[:], start=True, stop=False)
                with pe.Fori(0, NI) as i:
                    for k in range(2):
                        wait_apart(pe, hot_ready, 2 * i + k + 3, passed)
                        for c in range(COLS):
                            m = nc.tensor.matmul(count_p[:], hot[:, k, 0, c, :], hot[:, k, 1, c, :], start=False, stop=False)
                        m.then_inc(counted, 1)
                nc.tensor.matmul(count_p[:], ones[:], ones[:], start=False, stop=True).then_inc(summed, 1)
                pe.wait_ge(copied, 1)
                nc.tensor.matmul(sums_p[:, 0, :], g.ones[:], cnt[:], start=True, stop=True)
                nc.tensor.matmul(sums_p[:, 1, :], tri[:], cnt[:], start=True, stop=True).then_inc(summed, 1)

            @block.scalar
            def _(act):
                act.wait_ge(values_ready, 1)
                with act.Fori(0, NI) as i:
                    for k in range(2):
                        act.wait_ge(hot_ready, 2 * i + k + 1)
                        for side, values in enumerate((low, high)):
                            n = SPREAD[side]
                            m = nc.scalar.copy(spread[:, k, side, :n], bc(values[:, ds((2 * i + k) * COLS, n)], 2, P))
                        m.then_inc(spread_ready, 1)

            @block.sync
            def _(sp):
                sp.wait_ge(ends_ready, 1)
                with nc.allow_non_contiguous_dma(reason="two columns, turned"):
                    sp.dma_start(q.t_edge_dst.rearrange("two p -> p two"), ends[:]).then_inc(ends_out, 16)
                sp.wait_ge(ends_out, 16)

            @block.vector
            def _(v):
                vec = nc.vector
                link = chain(v, own)
                keys, dst = q.keys.bitcast(I32), q.dst.bitcast(I32)
                link(vec.tensor_scalar(dst, keys, NODE_BITS, LOW, ALU.logical_shift_right, ALU.bitwise_and))
                link(vec.tensor_scalar(low.bitcast(I32), dst, P - 1, None, ALU.bitwise_and))
                link(vec.tensor_copy(low, low.bitcast(I32)))
                link(vec.tensor_scalar(high.bitcast(I32), dst, 7, None, ALU.logical_shift_right))
                link(vec.tensor_copy(high, high.bitcast(I32)))
                link(vec.tensor_copy(ends[:, 0:1], dst[:, 0:1]))
                vec.tensor_copy(ends[:, 1:2], dst[:, ROW - 1:ROW]).then_inc(ends_ready, 1)
                v.wait_ge(made, 5)
                v.sem_inc(hot_ready, 2)
                v.sem_inc(values_ready, 1)
                with v.Fori(0, NI) as i:
                    for k in range(2):
                        v.wait_ge(counted, 2 * i + k + 1)
                        c = (2 * i + k) * COLS + SPREAD[1]
                        vec.tensor_tensor(hot[:, k, 1, SPREAD[1]:], lane[:, SPREAD[1]:],
                                          bc(high[:, ds(c, COLS - SPREAD[1])], 2, P), ALU.is_equal)
                        v.wait_ge(spread_ready, 2 * i + k + 1)
                        for side in range(2):
                            n = SPREAD[side]
                            m = vec.tensor_tensor(hot[:, k, side, :n], lane[:, :n], spread[:, k, side, :n], ALU.is_equal)
                        m.then_inc(hot_ready, 1)
                v.wait_ge(summed, 1)
                vec.tensor_copy(cnt[:], count_p[:]).then_inc(copied, 1)
                v.wait_ge(copied, 1)
                link(vec.tensor_scalar(has[:], cnt[:], 0.0, None, ALU.is_gt))
                v.wait_ge(summed, 2)
                link(vec.tensor_copy(tot[:], sums_p[:, 0, :]))
                link(vec.memset(b[:], 1.0))
                link(vec.tensor_tensor_scan(cum[:], b[:], tot[:], 0.0, ALU.mult, ALU.add))
                link(vec.tensor_tensor(cum[:], cum[:], tot[:], ALU.subtract))
                link(vec.tensor_tensor(start[:], cum[:], sums_p[:, 1, :], ALU.add))
                link(vec.tensor_tensor(end[:], start[:], cnt[:], ALU.add))
                link(vec.tensor_scalar(end[:], end[:], -1.0, None, ALU.add))
                link(vec.tensor_tensor(end[:], end[:], has[:], ALU.mult))
                link(vec.tensor_copy(ai[:], start[:]))
                link(vec.tensor_copy(bi[:], end[:]))
                link(vec.tensor_scalar(ai[:], ai[:], ROW.bit_length() - 1, None, ALU.logical_shift_right))
                link(vec.tensor_scalar(bi[:], bi[:], ROW.bit_length() - 1, None, ALU.logical_shift_right))
                link(vec.tensor_copy(a[:], ai[:]))
                link(vec.tensor_copy(b[:], bi[:]))
                link(vec.tensor_tensor(a[:], b[:], a[:], ALU.is_gt))
                link(vec.tensor_tensor(a[:], a[:], b[:], ALU.mult))
                link(vec.tensor_copy(q.carry_row[:], a[:]))
                link(vec.tensor_scalar(a[:], end[:], -float(EDGES), None, ALU.add))
                link(vec.tensor_tensor(a[:], a[:], has[:], ALU.mult))
                link(vec.tensor_scalar(a[:], a[:], float(EDGES), None, ALU.add))
                link(vec.tensor_copy(q.end_row[:], a[:]))
                link(vec.tensor_scalar(node[:], node[:], float(EDGES), None, ALU.add))
                link(vec.tensor_tensor(a[:], start[:], node[:], ALU.subtract))
                link(vec.tensor_tensor(a[:], a[:], has[:], ALU.mult))
                link(vec.tensor_tensor(a[:], a[:], node[:], ALU.add))
                link(vec.tensor_copy(q.start_row[:], a[:]))
                table_row(vec, link, q.first_row[:], ends[:, 0:1], first_tmp[:])
                link(vec.tensor_tensor(q.keep[:, 1:], dst[:, 1:], dst[:, :-1], ALU.is_equal))
                link(vec.memset(q.keep[:, 0:1], 0.0))
                table_row(vec, link, q.src_row.bitcast(I32), keys, dst)


def node_logits(nc, g, q, W, att_src, att_dst):
    with Stage(nc, "nodes") as st:
        w = st.sb("w", [P, CH])
        att = st.sb("att", [P, 2, CH])
        prod = st.sb("prod", [P, TILES, CH])
        zeros = st.sb("zeros", [P, (EDGES + TOKENS) * HEADS2 // P // 4])
        first = st.sb("first", [P, HEADS2])
        neutral = st.sb("neutral", [1, ST])
        hp = st.ps("h", [P, TILES, CH])
        own, loaded, cleared, full, tabled, out, zeroed, scattered, gathered, firsts_out = (
            st.sem(n) for n in ("vec_own", "loaded", "cleared", "full", "tabled", "out", "zeroed", "scattered",
                                "gathered", "firsts_out"))
        with nc.Block() as block:
            @block.sync
            def _(sp):
                sp.dma_start(w[0:D, :], W).then_inc(loaded, 16)
                for n, t in enumerate((att_src, att_dst)):
                    sp.dma_start(att[:, n, :], t.rearrange("h e -> (h e)").partition_broadcast(P)).then_inc(loaded, 16)
                sp.wait_ge(cleared, 4)
                starts = q.t_starts.rearrange("(p m) c -> p (m c)", p=P)
                step = zeros.shape[1]
                for n in range(4):
                    sp.dma_start(starts[:, n * step:(n + 1) * step], zeros[:]).then_inc(zeroed, 16)
                sp.dma_start(q.t_state[EDGES:EDGES + 1, :], neutral[:]).then_inc(out, 16)
                sp.wait_ge(tabled, 2)
                sp.dma_start(q.t_table.rearrange("(p t) c -> p t c", p=P), q.table[:]).then_inc(out, 16)
                sp.dma_start(q.t_dst.rearrange("(p t) c -> p t c", p=P), q.a_dst[:]).then_inc(out, 16)
                sp.wait_ge(out, 48)
                sp.wait_ge(gathered, 16)
                sp.wait_ge(scattered, 16 * TILES)
                sp.dma_start(q.t_starts[0:EDGES, :].rearrange("(p f) c -> p f c", p=P)[:, 0, :], first[:]).then_inc(firsts_out, 16)
                sp.wait_ge(firsts_out, 16)

            @block.tensor
            def _(pe):
                pe.wait_ge(loaded, 48)
                pe.wait_ge(cleared, 4)
                for t in range(TILES):
                    m = nc.tensor.matmul(hp[:, t, :], g.XT[:, t * P:(t + 1) * P], w[:], start=True, stop=True)
                m.then_inc(full, 1)

            @block.vector
            def _(v):
                vec = nc.vector
                link = chain(v, own)
                vec.memset(w[D:P, :], 0.0).then_inc(cleared, 1)
                vec.memset(zeros[:], 0.0).then_inc(cleared, 1)
                vec.memset(neutral[:, HEADS2:], 0.0).then_inc(cleared, 1)
                vec.memset(neutral[:, 0:HEADS2], -BIG).then_inc(cleared, 1)
                v.wait_ge(full, 1)
                v.wait_ge(loaded, 48)
                h = q.table[:, :, 0:CH]
                link(vec.tensor_copy(h, hp[:]))
                for n, logits in enumerate((q.table[:, :, CH:TAB], q.a_dst[:])):
                    link(vec.tensor_tensor(prod[:], h, bc(att[:, n, :], 1, TILES), ALU.mult))
                    vec.reduce_sum(logits, prod[:].rearrange("p t (h e) -> p t h e", h=HEADS2), AX.X).then_inc(tabled, 1)
                    v.wait_ge(tabled, n + 1)

            @block.gpsimd
            def _(pool):
                pool.wait_ge(tabled, 2)
                pool.wait_ge(zeroed, 64)
                for t in range(TILES):
                    nc.gpsimd.indirect_dma_start(
                        out=q.t_starts, out_offset=bass.IndirectOffsetOnAxis(ap=q.start_row[:, t:t + 1], axis=0),
                        in_=q.a_dst[:, t, :], in_offset=None).then_inc(scattered, 16)
                pool.wait_ge(out, 48)
                nc.gpsimd.indirect_dma_start(
                    out=first[:], out_offset=None, in_=q.t_dst,
                    in_offset=bass.IndirectOffsetOnAxis(ap=q.first_row[:], axis=0)).then_inc(gathered, 16)
                pool.wait_ge(gathered, 16)


class RunningSoftmax:

    def __init__(self, st, parts, C):
        self.C = C
        self.diff = st.sb("diff", [parts, 2, C, HEADS2])
        self.reset = st.sb("reset", [parts, C])
        self.decay = st.sb("decay", [parts, C, HEADS2])
        self.addend = st.sb("addend", [parts, C, HEADS2 + CH])

    def maxima(self, v, link, out, before, e, keep):
        C = self.C
        link(v.tensor_scalar(self.reset[:], keep, -1.0, BIG, ALU.add, ALU.mult))
        for h in range(HEADS2):
            m = v.tensor_tensor_scan(out[:, :, h], self.reset[:], e[:, :, h], before[:, h:h + 1], ALU.add, ALU.max)
        link(m)
        v.tensor_tensor(self.diff[:, 0], e, out[:, :, 0:HEADS2], ALU.subtract)
        v.tensor_tensor(self.diff[:, 1, 0, :], before[:, 0:HEADS2], out[:, 0, 0:HEADS2], ALU.subtract)
        link(v.tensor_tensor(self.diff[:, 1, 1:], out[:, 0:C - 1, 0:HEADS2], out[:, 1:C, 0:HEADS2], ALU.subtract))
        return v.tensor_scalar(self.diff[:, 1], self.diff[:, 1], 0.0, None, ALU.min)

    def sums(self, v, link, out, before, keep, values, weights=None):
        C = self.C
        v.tensor_tensor(self.decay[:], self.diff[:, 1], bc(keep, 2, HEADS2), ALU.mult)
        w = self.diff[:, 0]
        if weights is None:
            v.tensor_copy(self.addend[:, :, 0:HEADS2], w)
        else:
            v.tensor_tensor(self.addend[:, :, 0:HEADS2], w, weights, ALU.mult)
        for h in range(HEADS2):
            m = v.tensor_tensor(self.addend[:, :, HEADS2 + 4 * h:HEADS2 + 4 * h + 4], values[:, :, 4 * h:4 * h + 4],
                                bc(w[:, :, h], 2, 4), ALU.mult)
        link(m)
        for c in range(HEADS2 + CH):
            h = c if c < HEADS2 else (c - HEADS2) // 4
            m = v.tensor_tensor_scan(out[:, :, HEADS2 + c], self.decay[:, :, h], self.addend[:, :, c],
                                     before[:, HEADS2 + c:HEADS2 + c + 1], ALU.mult, ALU.add)
        return m


def leaky(v, out, x):
    return v.scalar_tensor_tensor(out, x, 0.2, x, ALU.mult, ALU.max)


def edge_softmax(nc, g, q):
    C = 64
    NI = ROW // (2 * C)
    with Stage(nc, "edges") as st:
        flat = g.X[:].rearrange("p t d -> p (t d)")
        rows = flat[:, 0:2 * C * TAB].rearrange("p (k c r) -> p k c r", k=2, r=TAB)
        starts = st.sb("starts", [P, 2, C, HEADS2])
        idx, keep = st.sb("idx", [P, 2, C], I32), st.sb("keep", [P, 2, C])
        a_dst, e = st.sb("a_dst", [P, C, HEADS2]), st.sb("e", [P, C, HEADS2])
        last_dst = st.sb("last_dst", [P, HEADS2])
        state = g.GT[:].bitcast(F32)[:, 0:2 * C * ST].rearrange("p (k c r) -> p k c r", k=2, r=ST)
        soft = RunningSoftmax(st, P, C)
        own, idx_ready, rows_used, passed, diff_ready, exped, state_ready, starts_used = (
            st.sem(n) for n in ("vec_own", "idx_ready", "rows_used", "pool_passed", "diff_ready", "exped",
                                "state_ready", "starts_used"))
        gathered, starts_in, stored = ([st.sem(f"{n}{k}") for k in range(2)] for n in ("gathered", "starts_in", "stored"))
        with nc.Block() as block:
            @block.sync
            def _(sp):
                src = q.t_starts[0:EDGES, :].rearrange("(p f) c -> p f c", p=P)
                dst = q.t_state[0:EDGES, :].rearrange("(p f) c -> p f c", p=P)
                sp.sem_inc(stored[0], 16)
                sp.sem_inc(stored[1], 16)
                with sp.Fori(0, NI) as i:
                    for k in range(2):
                        sp.wait_ge(starts_used, 2 * i + k + 1)
                        sp.dma_start(starts[:, k], src[:, ds((2 * i + k) * C, C), :]).then_inc(starts_in[k], 16)
                    for k in range(2):
                        sp.wait_ge(state_ready, 2 * i + k + 1)
                        sp.dma_start(dst[:, ds((2 * i + k) * C, C), :], state[:, k]).then_inc(stored[k], 16)
                for k in range(2):
                    sp.wait_ge(stored[k], 16 * (NI + 1))

            @block.gpsimd
            def _(pool):
                with pool.Fori(0, NI) as i:
                    for k in range(2):
                        pool.wait_ge(idx_ready, 2 * i + k + 1)
                        wait_apart(pool, rows_used, 2 * i + k + 1, passed)
                        for c in range(C):
                            nc.gpsimd.indirect_dma_start(
                                out=rows[:, k, c, :], out_offset=None, in_=q.t_table,
                                in_offset=bass.IndirectOffsetOnAxis(ap=idx[:, k, c:c + 1], axis=0)).then_inc(gathered[k], 16)

            @block.scalar
            def _(act):
                with act.Fori(0, NI) as i:
                    for k in range(2):
                        act.wait_ge(diff_ready, 2 * i + k + 1)
                        nc.scalar.activation(soft.diff[:], soft.diff[:], ACT.Exp).then_inc(exped, 1)

            @block.vector
            def _(v):
                vec = nc.vector
                PER = 7
                vec.memset(last_dst[:], 0.0).then_inc(own, 1)
                vec.memset(state[:, 1, C - 1, HEADS2:], 0.0).then_inc(own, 1)
                vec.memset(state[:, 1, C - 1, 0:HEADS2], -BIG).then_inc(own, 1)
                v.sem_inc(rows_used, 2)
                v.sem_inc(starts_used, 2)
                BEFORE = 3

                def fetch(c, k):
                    return vec.tensor_copy(idx[:, k], q.src_row.bitcast(I32)[:, ds(c * C, C)])

                for k in range(2):
                    fetch(k, k).then_inc(idx_ready, 1)
                v.wait_ge(own, BEFORE)

                def chunk(c, k, i, ahead):
                    turn = 2 * i + k
                    link = chain(v, own, turn, PER, BEFORE)

                    def rows_done(ins):
                        ins.then_inc(rows_used, 1)
                        v.wait_ge(rows_used, turn + 3)

                    link(vec.tensor_copy(keep[:, k], q.keep[:, ds(c * C, C)]))
                    v.wait_ge(starts_in[k], 16 * i + 16)
                    for h in range(HEADS2):
                        m = vec.tensor_tensor_scan(a_dst[:, :, h], keep[:, k], starts[:, k, :, h], last_dst[:, h:h + 1],
                                                   ALU.mult, ALU.add)
                    m.then_inc(starts_used, 1)
                    v.wait_ge(starts_used, turn + 3)
                    v.wait_ge(gathered[k], 16 * C * i + 16 * C)
                    if ahead:
                        fetch(c + 2, k).then_inc(idx_ready, 1)
                    link(vec.tensor_copy(last_dst[:], a_dst[:, C - 1, :]))
                    link(vec.tensor_tensor(e[:], rows[:, k, :, CH:TAB], a_dst[:], ALU.add))
                    link(leaky(vec, e[:], e[:]))
                    v.wait_ge(stored[k], 16 * i + 16)
                    before = state[:, 1 - k, C - 1, :]
                    soft.maxima(vec, link, state[:, k], before, e[:], keep[:, k]).then_inc(diff_ready, 1)
                    v.wait_ge(exped, turn + 1)
                    soft.sums(vec, rows_done, state[:, k], before, keep[:, k], rows[:, k]).then_inc(state_ready, 1)
                    v.wait_ge(state_ready, turn + 1)
                    assert link.count[0] == PER

                with v.Fori(0, NI - 1) as i:
                    for k in range(2):
                        chunk(2 * i + k, k, i, True)
                for k in range(2):
                    chunk(2 * (NI - 1) + k, k, NI - 1, False)


def carry_states(nc, g, q):
    with Stage(nc, "carry") as st:
        flat = g.X[0:1].rearrange("p t d -> p (t d)")
        tails = flat[:, 0:P * ST].rearrange("p (r c) -> p r c", c=ST)
        states = flat[:, P * ST:(2 * P + 1) * ST].rearrange("p (r c) -> p r c", c=ST)
        ends = st.sb("ends", [1, 2, P], I32)
        whole, cont = st.sb("whole", [1, P]), st.sb("cont", [1, P])
        soft = RunningSoftmax(st, 1, P)
        loaded, stored, own, diff_ready, exped, done = (
            st.sem(n) for n in ("loaded", "stored", "vec_own", "diff_ready", "exped", "done"))
        with nc.Block() as block:
            @block.sync
            def _(sp):
                last = q.t_state[0:EDGES, :].rearrange("(p f) c -> p f c", p=P)[:, ROW - 1, :]
                sp.dma_start(tails, last.unsqueeze(0)).then_inc(loaded, 16)
                sp.dma_start(ends[:], q.t_edge_dst.unsqueeze(0)).then_inc(loaded, 16)
                sp.wait_ge(done, 1)
                sp.dma_start(q.t_carry.unsqueeze(0), states[:, 0:P, :]).then_inc(stored, 16)
                sp.wait_ge(stored, 16)

            @block.scalar
            def _(act):
                act.wait_ge(diff_ready, 1)
                nc.scalar.activation(soft.diff[:], soft.diff[:], ACT.Exp).then_inc(exped, 1)

            @block.vector
            def _(v):
                vec = nc.vector
                link = chain(v, own)
                link(vec.memset(states[:, 0, :], 0.0))
                link(vec.memset(states[:, 0, 0:HEADS2], -BIG))
                link(vec.memset(cont[:], 0.0))
                v.wait_ge(loaded, 32)
                link(vec.tensor_tensor(whole[:], ends[:, 0, :], ends[:, 1, :], ALU.is_equal))
                link(vec.tensor_tensor(cont[:, 1:], ends[:, 0, 1:], ends[:, 1, :-1], ALU.is_equal))
                link(vec.tensor_tensor(cont[:], cont[:], whole[:], ALU.mult))
                out = states[:, 1:, :]
                soft.maxima(vec, link, out, states[:, 0, :], tails[:, :, 0:HEADS2], cont[:]).then_inc(diff_ready, 1)
                v.wait_ge(exped, 1)
                soft.sums(vec, link, out, states[:, 0, :], cont[:], tails[:, :, 2 * HEADS2:],
                          weights=tails[:, :, HEADS2:2 * HEADS2]).then_inc(done, 1)
                v.wait_ge(done, 1)


def node_gates(nc, g, q, b_gat, gamma, beta):
    E = 4
    with Stage(nc, "gates") as st:
        flat = g.X[:].rearrange("p t d -> p (t d)")
        run = flat[:, 0:TILES * ST].rearrange("p (t c) -> p t c", c=ST)
        carry = flat[:, TILES * ST:2 * TILES * ST].rearrange("p (t c) -> p t c", c=ST)
        diff = st.sb("diff", [P, 3, TILES, HEADS2])
        m, den = st.sb("m", [P, TILES, HEADS2]), st.sb("den", [P, TILES, HEADS2])
        num = st.sb("num", [P, TILES, CH])
        part = flat[:, 2 * TILES * ST:2 * TILES * ST + TILES * CH].rearrange("p (t c) -> p t c", c=CH)
        params = st.sb("params", [P, 3, CH])
        mean = st.sb("mean", [P, TILES])
        L, G, hot, tmp = (st.sb(n, [P, TILES, E]) for n in ("L", "G", "hot", "tmp"))
        own, loaded, gathered, diff_ready, exped, var_ready, std_ready = (
            st.sem(n) for n in ("vec_own", "loaded", "gathered", "diff_ready", "exped", "var_ready", "std_ready"))
        gates = GateSplit(nc, g, st, E, tmp[:])
        with nc.Block() as block:
            parts = {}

            @block.sync
            def _(sp):
                for n, t in enumerate((b_gat, gamma, beta)):
                    sp.dma_start(params[:, n, :], t.partition_broadcast(P)).then_inc(loaded, 16)

            @block.vector
            def _(v):
                vec = nc.vector
                link = chain(v, own)
                own_e = diff[:, 2]
                link(vec.tensor_tensor(own_e, q.table[:, :, CH:TAB], q.a_dst[:], ALU.add))
                link(leaky(vec, own_e, own_e))
                v.wait_ge(gathered, 2 * 16 * TILES)
                v.wait_ge(loaded, 48)
                link(vec.tensor_tensor(m[:], run[:, :, 0:HEADS2], carry[:, :, 0:HEADS2], ALU.max))
                link(vec.tensor_tensor(m[:], m[:], own_e, ALU.max))
                link(vec.tensor_tensor(diff[:, 0], run[:, :, 0:HEADS2], m[:], ALU.subtract))
                link(vec.tensor_tensor(diff[:, 1], carry[:, :, 0:HEADS2], m[:], ALU.subtract))
                vec.tensor_tensor(own_e, own_e, m[:], ALU.subtract).then_inc(diff_ready, 1)
                v.wait_ge(exped, 1)
                link(vec.tensor_tensor(m[:], diff[:, 0], run[:, :, HEADS2:2 * HEADS2], ALU.mult))
                link(vec.tensor_tensor(den[:], diff[:, 1], carry[:, :, HEADS2:2 * HEADS2], ALU.mult))
                link(vec.tensor_tensor(den[:], den[:], m[:], ALU.add))
                link(vec.tensor_tensor(den[:], den[:], own_e, ALU.add))
                link(vec.tensor_scalar(den[:], den[:], 1e-16, None, ALU.add))
                link(vec.reciprocal(den[:], den[:]))
                for n, values in enumerate((run[:, :, 2 * HEADS2:], carry[:, :, 2 * HEADS2:], q.table[:, :, 0:CH])):
                    to = part if n else num[:]
                    for h in range(HEADS2):
                        c = slice(4 * h, 4 * h + 4)
                        link(vec.tensor_tensor(to[:, :, c], values[:, :, c], bc(diff[:, n, :, h], 2, 4), ALU.mult))
                    if n:
                        link(vec.tensor_tensor(num[:], num[:], part, ALU.add))
                for h in range(HEADS2):
                    c = slice(4 * h, 4 * h + 4)
                    link(vec.tensor_tensor(num[:, :, c], num[:, :, c], bc(den[:, :, h], 2, 4), ALU.mult))
                link(vec.tensor_tensor(num[:], num[:], bc(params[:, 0], 1, TILES), ALU.add))
                link(vec.reduce_sum(mean[:], num[:], AX.X))
                link(vec.tensor_scalar(mean[:], mean[:], 1.0 / CH, None, ALU.mult))
                link(vec.tensor_tensor(num[:], num[:], bc(mean[:], 2, CH), ALU.subtract))
                link(vec.tensor_tensor(part, num[:], num[:], ALU.mult))
                vec.reduce_sum(mean[:], part, AX.X).then_inc(var_ready, 1)
                v.wait_ge(std_ready, 1)
                link(vec.reciprocal(mean[:], mean[:]))
                link(vec.tensor_tensor(num[:], num[:], bc(mean[:], 2, CH), ALU.mult))
                link(vec.tensor_tensor(num[:], num[:], bc(params[:, 1], 1, TILES), ALU.mult))
                link(vec.tensor_tensor(num[:], num[:], bc(params[:, 2], 1, TILES), ALU.add))
                link(vec.reduce_sum(L[:], num[:].rearrange("p t (h e) -> p t e h", h=HEADS2), AX.X))
                link(vec.tensor_scalar(L[:], L[:], 1.0 / HEADS2, None, ALU.mult))
                steps, parts["pool"], parts["act"] = top2_steps(nc, v, link, st, L[:], G[:], E, hot[:], tmp[:])
                steps()
                gates.vector(link, G[:])

            @block.scalar
            def _(act):
                act.wait_ge(diff_ready, 1)
                nc.scalar.activation(diff[:], diff[:], ACT.Exp).then_inc(exped, 1)
                act.wait_ge(var_ready, 1)
                nc.scalar.activation(mean[:], mean[:], ACT.Sqrt, bias=g.eps[:], scale=1.0 / CH).then_inc(std_ready, 1)
                parts["act"](act)
                gates.scalar(act)

            @block.gpsimd
            def _(pool):
                for t in range(TILES):
                    for out, table, rows in ((run, q.t_state, q.end_row), (carry, q.t_carry, q.carry_row)):
                        nc.gpsimd.indirect_dma_start(
                            out=out[:, t, :], out_offset=None, in_=table,
                            in_offset=bass.IndirectOffsetOnAxis(ap=rows[:, t:t + 1], axis=0)).then_inc(gathered, 16)
                parts["pool"](pool)
                gates.gpsimd()

            @block.tensor
            def _(pe):
                gates.tensor(pe)


def ffn2(nc, g, I):
    with ExitStack() as ctx:
        q = Gat(nc, g, ctx)
        sort_edges(nc, g, q.keys, I["L2_ffn_edge_index"])
        locate_runs(nc, g, q)
        layernorm(nc, g, "ln_f2", g.H, transposed=True)
        node_logits(nc, g, q, I["L2_ffn_W_gat"], I["L2_ffn_att_src"], I["L2_ffn_att_dst"])
        edge_softmax(nc, g, q)
        carry_states(nc, g, q)
        node_gates(nc, g, q, I["L2_ffn_b_gat"], I["L2_ffn_ln_gamma"], I["L2_ffn_ln_beta"])
    experts(nc, g, "experts2", I["L2_ffn_W1"], I["L2_ffn_W2"], I["L2_ffn_b1"], I["L2_ffn_b2"], target=g.H)


def forward(nc, g, I, out):
    ids = [I[k] for k in ("x", "itok_BS_0_255", "itok_BS_0_511", "itok_BS_0_127", "itok_BS_0_63", "itok_BS_0_3")]
    tables = [I["L0_tok_E_" + k] for k in ("et", "fc", "sc", "of", "tt", "rc")]
    constants(nc, g)
    embed(nc, g, ids, tables, I["L0_tok_W"], I["L0_tok_b"])
    layernorm(nc, g, "ln_tok", g.H, I["L0_tok_gamma"], I["L0_tok_beta"], keep=g.H)
    attn0(nc, g, I)
    layernorm(nc, g, "ln_f0", g.H, keep=g.X)
    layernorm(nc, g, "ln_in0", g.X, I["L0_ffn_gamma"], I["L0_ffn_beta"], transposed=True)
    route(nc, g, "route0", I["L0_ffn_Wr"], I["L0_ffn_br"], 8)
    experts(nc, g, "experts0", I["L0_ffn_W1"], I["L0_ffn_W2"], I["L0_ffn_b1"], I["L0_ffn_b2"], target=g.H)
    attn1(nc, g, I)
    ffn1(nc, g, I)
    attn2(nc, g, I)
    ffn2(nc, g, I)
    attn3(nc, g, I)
    layernorm(nc, g, "ln_f3", g.H, transposed=True)
    route(nc, g, "route3", I["L3_ffn_gate_w"], I["L3_ffn_gate_b"], 16, probs=True)
    experts(nc, g, "experts3", I["L3_ffn_w1"], I["L3_ffn_w3"], Wg=I["L3_ffn_w2"], target=g.H)
    store(nc, g, out)


def tower(nc, I, out):
    with ExitStack() as ctx:
        forward(nc, allocate(nc, ctx), I, out)


_INS = ['x', 'itok_BS_0_255', 'itok_BS_0_511', 'itok_BS_0_127', 'itok_BS_0_63', 'itok_BS_0_3', 'L0_tok_E_et',
        'L0_tok_E_fc', 'L0_tok_E_sc', 'L0_tok_E_of', 'L0_tok_E_tt', 'L0_tok_E_rc', 'L0_tok_W', 'L0_tok_b',
        'L0_tok_gamma', 'L0_tok_beta', 'L0_attn_Wq', 'L0_attn_Wk', 'L0_ffn_gamma', 'L0_ffn_beta', 'L0_ffn_Wr',
        'L0_ffn_br', 'L0_ffn_W1', 'L0_ffn_b1', 'L0_ffn_W2', 'L0_ffn_b2', 'L1_attn_w_qkv', 'L1_attn_b_qkv',
        'L1_attn_w_proj', 'L1_attn_b_proj', 'L1_ffn_Wr', 'L1_ffn_br', 'L1_ffn_W1', 'L1_ffn_b1', 'L1_ffn_W2',
        'L1_ffn_b2', 'L1_ffn_gamma', 'L1_ffn_beta', 'L2_attn_WQ', 'L2_attn_WK', 'L2_attn_WV', 'L2_attn_Wout',
        'L2_attn_bout', 'L2_ffn_W_gat', 'L2_ffn_att_src', 'L2_ffn_att_dst', 'L2_ffn_b_gat', 'L2_ffn_ln_gamma',
        'L2_ffn_ln_beta', 'L2_ffn_W1', 'L2_ffn_b1', 'L2_ffn_W2', 'L2_ffn_b2', 'L2_ffn_edge_index', 'L3_attn_w_qkv',
        'L3_attn_w_proj', 'L3_attn_b_proj', 'L3_attn_slopes', 'L3_ffn_gate_w', 'L3_ffn_gate_b', 'L3_ffn_w1',
        'L3_ffn_w2', 'L3_ffn_w3']


def kernel(**inputs):
    import numpy as _np
    import concourse.bacc as _bacc
    from concourse import mybir as _mybir
    from concourse.bass_utils import run_bass_kernel_spmd as _run

    nc = _bacc.Bacc("TRN2", target_bir_lowering=False, num_devices=1)
    arrays, args = {}, {}
    for name in _INS:
        a = _np.ascontiguousarray(inputs[name])
        arrays[f"in_{name}_dram"] = a
        args[name] = nc.dram_tensor(f"in_{name}_dram", a.shape, _mybir.dt.from_np(a.dtype), kind="ExternalInput").ap()
    out = nc.dram_tensor("out_0_dram", (B, S, D), _mybir.dt.float32, kind="ExternalOutput").ap()
    tower(nc, args, out)
    r = _run(nc, [arrays], core_ids=[0])
    return r.results[0]["out_0_dram"]
```
